# Optimizing a Trainium2 kernel written in Bass

```python
import numpy as np
import jax
import jax.numpy as jnp

def _softmax(x, axis=-1):
    return jax.nn.softmax(x, axis=axis)

def _gelu(x):
    return jax.nn.gelu(x, approximate=True)

def _silu(x):
    return jax.nn.silu(x)

def _sigmoid(x):
    return jax.nn.sigmoid(x)

def _layernorm(x, axis=-1, eps=1e-05):
    m = jnp.mean(x, axis=axis, keepdims=True)
    v = jnp.var(x, axis=axis, keepdims=True)
    return (x - m) / jnp.sqrt(v + eps)

def _scatter_add(tgt, idx, src, axis=0):
    return tgt.at[idx].add(src)

def _segment_sum(src, seg, n):
    return jax.ops.segment_sum(src, seg, n)
kernel_name = 'mk_dlrm_tower_d1_rec_r8_456d15'

def setup_inputs(seed: int=0):
    np.random.seed(seed)
    _w = jnp.asarray

    def _rec_inputs():
        import jax
        import jax.numpy as jnp
        _tk = jax.random.key(seed)
        dense_ctx = jax.random.normal(jax.random.fold_in(_tk, 190), (2048, 16), jnp.float32)
        ids = jnp.stack([jax.random.randint(jax.random.fold_in(_tk, 200 + f), (2048,), 0, v, jnp.int32) for f, v in enumerate([1000, 1000, 12500, 1000, 12500, 1250, 1000, 12500, 1000, 125000, 125000, 12500, 12500, 125000, 125000, 125000, 1250, 1000, 12500, 12500, 1000, 1250, 125000, 1250, 1250, 12500, 1000, 125000, 125000, 1000, 125000, 125000, 1250, 1250, 1000, 125000, 1000, 125000, 1000])], axis=1)
        tbl_0 = 0.05 * jax.random.normal(jax.random.fold_in(_tk, 500 + 0), (1000, 16), jnp.float32)
        tbl_1 = 0.05 * jax.random.normal(jax.random.fold_in(_tk, 500 + 1), (1000, 16), jnp.float32)
        tbl_2 = 0.05 * jax.random.normal(jax.random.fold_in(_tk, 500 + 2), (12500, 16), jnp.float32)
        tbl_3 = 0.05 * jax.random.normal(jax.random.fold_in(_tk, 500 + 3), (1000, 16), jnp.float32)
        tbl_4 = 0.05 * jax.random.normal(jax.random.fold_in(_tk, 500 + 4), (12500, 16), jnp.float32)
        tbl_5 = 0.05 * jax.random.normal(jax.random.fold_in(_tk, 500 + 5), (1250, 16), jnp.float32)
        tbl_6 = 0.05 * jax.random.normal(jax.random.fold_in(_tk, 500 + 6), (1000, 16), jnp.float32)
        tbl_7 = 0.05 * jax.random.normal(jax.random.fold_in(_tk, 500 + 7), (12500, 16), jnp.float32)
        tbl_8 = 0.05 * jax.random.normal(jax.random.fold_in(_tk, 500 + 8), (1000, 16), jnp.float32)
        tbl_9 = 0.05 * jax.random.normal(jax.random.fold_in(_tk, 500 + 9), (125000, 16), jnp.float32)
        tbl_10 = 0.05 * jax.random.normal(jax.random.fold_in(_tk, 500 + 10), (125000, 16), jnp.float32)
        tbl_11 = 0.05 * jax.random.normal(jax.random.fold_in(_tk, 500 + 11), (12500, 16), jnp.float32)
        tbl_12 = 0.05 * jax.random.normal(jax.random.fold_in(_tk, 500 + 12), (12500, 16), jnp.float32)
        tbl_13 = 0.05 * jax.random.normal(jax.random.fold_in(_tk, 500 + 13), (125000, 16), jnp.float32)
        tbl_14 = 0.05 * jax.random.normal(jax.random.fold_in(_tk, 500 + 14), (125000, 16), jnp.float32)
        tbl_15 = 0.05 * jax.random.normal(jax.random.fold_in(_tk, 500 + 15), (125000, 16), jnp.float32)
        tbl_16 = 0.05 * jax.random.normal(jax.random.fold_in(_tk, 500 + 16), (1250, 16), jnp.float32)
        tbl_17 = 0.05 * jax.random.normal(jax.random.fold_in(_tk, 500 + 17), (1000, 16), jnp.float32)
        tbl_18 = 0.05 * jax.random.normal(jax.random.fold_in(_tk, 500 + 18), (12500, 16), jnp.float32)
        tbl_19 = 0.05 * jax.random.normal(jax.random.fold_in(_tk, 500 + 19), (12500, 16), jnp.float32)
        tbl_20 = 0.05 * jax.random.normal(jax.random.fold_in(_tk, 500 + 20), (1000, 16), jnp.float32)
        tbl_21 = 0.05 * jax.random.normal(jax.random.fold_in(_tk, 500 + 21), (1250, 16), jnp.float32)
        tbl_22 = 0.05 * jax.random.normal(jax.random.fold_in(_tk, 500 + 22), (125000, 16), jnp.float32)
        tbl_23 = 0.05 * jax.random.normal(jax.random.fold_in(_tk, 500 + 23), (1250, 16), jnp.float32)
        tbl_24 = 0.05 * jax.random.normal(jax.random.fold_in(_tk, 500 + 24), (1250, 16), jnp.float32)
        tbl_25 = 0.05 * jax.random.normal(jax.random.fold_in(_tk, 500 + 25), (12500, 16), jnp.float32)
        tbl_26 = 0.05 * jax.random.normal(jax.random.fold_in(_tk, 500 + 26), (1000, 16), jnp.float32)
        tbl_27 = 0.05 * jax.random.normal(jax.random.fold_in(_tk, 500 + 27), (125000, 16), jnp.float32)
        tbl_28 = 0.05 * jax.random.normal(jax.random.fold_in(_tk, 500 + 28), (125000, 16), jnp.float32)
        tbl_29 = 0.05 * jax.random.normal(jax.random.fold_in(_tk, 500 + 29), (1000, 16), jnp.float32)
        tbl_30 = 0.05 * jax.random.normal(jax.random.fold_in(_tk, 500 + 30), (125000, 16), jnp.float32)
        tbl_31 = 0.05 * jax.random.normal(jax.random.fold_in(_tk, 500 + 31), (125000, 16), jnp.float32)
        tbl_32 = 0.05 * jax.random.normal(jax.random.fold_in(_tk, 500 + 32), (1250, 16), jnp.float32)
        tbl_33 = 0.05 * jax.random.normal(jax.random.fold_in(_tk, 500 + 33), (1250, 16), jnp.float32)
        tbl_34 = 0.05 * jax.random.normal(jax.random.fold_in(_tk, 500 + 34), (1000, 16), jnp.float32)
        tbl_35 = 0.05 * jax.random.normal(jax.random.fold_in(_tk, 500 + 35), (125000, 16), jnp.float32)
        tbl_36 = 0.05 * jax.random.normal(jax.random.fold_in(_tk, 500 + 36), (1000, 16), jnp.float32)
        tbl_37 = 0.05 * jax.random.normal(jax.random.fold_in(_tk, 500 + 37), (125000, 16), jnp.float32)
        tbl_38 = 0.05 * jax.random.normal(jax.random.fold_in(_tk, 500 + 38), (1000, 16), jnp.float32)
        _rk = jax.random.fold_in(_tk, 7)
        W_top1 = 0.0693375 * jax.random.normal(jax.random.fold_in(_tk, 801), (208, 512), jnp.float32)
        W_top2 = 0.0441942 * jax.random.normal(jax.random.fold_in(_tk, 802), (512, 256), jnp.float32)
        W_top3 = 0.0625 * jax.random.normal(jax.random.fold_in(_tk, 803), (256, 1), jnp.float32)
        b_top1 = jnp.zeros((512,), jnp.float32)
        b_top2 = jnp.zeros((256,), jnp.float32)
        return (dense_ctx, ids, tbl_0, tbl_1, tbl_2, tbl_3, tbl_4, tbl_5, tbl_6, tbl_7, tbl_8, tbl_9, tbl_10, tbl_11, tbl_12, tbl_13, tbl_14, tbl_15, tbl_16, tbl_17, tbl_18, tbl_19, tbl_20, tbl_21, tbl_22, tbl_23, tbl_24, tbl_25, tbl_26, tbl_27, tbl_28, tbl_29, tbl_30, tbl_31, tbl_32, tbl_33, tbl_34, tbl_35, tbl_36, tbl_37, tbl_38, W_top1, b_top1, W_top2, b_top2, W_top3)
    dense_ctx, ids, tbl_0, tbl_1, tbl_2, tbl_3, tbl_4, tbl_5, tbl_6, tbl_7, tbl_8, tbl_9, tbl_10, tbl_11, tbl_12, tbl_13, tbl_14, tbl_15, tbl_16, tbl_17, tbl_18, tbl_19, tbl_20, tbl_21, tbl_22, tbl_23, tbl_24, tbl_25, tbl_26, tbl_27, tbl_28, tbl_29, tbl_30, tbl_31, tbl_32, tbl_33, tbl_34, tbl_35, tbl_36, tbl_37, tbl_38, W_top1, b_top1, W_top2, b_top2, W_top3 = _rec_inputs()

    def _L0_rec_setup():
        import jax, jax.numpy as jnp
        import numpy as np
        B, F, D = (512, 39, 16)
        L0, L1 = (128, 128)
        H1 = L0 // 2

        def _cin_layer(h, h0, W, b):
            z = jnp.einsum('bhd,bmd->bhmd', h, h0)
            z = z.reshape(z.shape[0], -1, z.shape[-1])
            y = jnp.einsum('oc,bcd->bod', W, z) + b[None, :, None]
            return jax.nn.relu(y)
        key = jax.random.key(seed)
        k0, k1, k2, k3, k4 = jax.random.split(key, 5)
        x = jax.random.normal(k0, (B, F, D), dtype=jnp.float32)
        W0 = jax.random.normal(k1, (L0, F * F), dtype=jnp.float32) * 0.02
        b0 = jnp.zeros((L0,), dtype=jnp.float32)
        W1 = jax.random.normal(k2, (L1, H1 * F), dtype=jnp.float32) * 0.02
        b1 = jnp.zeros((L1,), dtype=jnp.float32)
        return {'x': x, 'W0': W0, 'b0': b0, 'W1': W1, 'b1': b1}
    _L0_rec_all = _L0_rec_setup()
    _L0_rec_in = {k: v for k, v in _L0_rec_all.items() if k in ('W0', 'b0', 'W1', 'b1')}
    del _L0_rec_all
    return {'dense_ctx': dense_ctx, 'ids': ids, 'tbl_0': tbl_0, 'tbl_1': tbl_1, 'tbl_2': tbl_2, 'tbl_3': tbl_3, 'tbl_4': tbl_4, 'tbl_5': tbl_5, 'tbl_6': tbl_6, 'tbl_7': tbl_7, 'tbl_8': tbl_8, 'tbl_9': tbl_9, 'tbl_10': tbl_10, 'tbl_11': tbl_11, 'tbl_12': tbl_12, 'tbl_13': tbl_13, 'tbl_14': tbl_14, 'tbl_15': tbl_15, 'tbl_16': tbl_16, 'tbl_17': tbl_17, 'tbl_18': tbl_18, 'tbl_19': tbl_19, 'tbl_20': tbl_20, 'tbl_21': tbl_21, 'tbl_22': tbl_22, 'tbl_23': tbl_23, 'tbl_24': tbl_24, 'tbl_25': tbl_25, 'tbl_26': tbl_26, 'tbl_27': tbl_27, 'tbl_28': tbl_28, 'tbl_29': tbl_29, 'tbl_30': tbl_30, 'tbl_31': tbl_31, 'tbl_32': tbl_32, 'tbl_33': tbl_33, 'tbl_34': tbl_34, 'tbl_35': tbl_35, 'tbl_36': tbl_36, 'tbl_37': tbl_37, 'tbl_38': tbl_38, 'W_top1': W_top1, 'b_top1': b_top1, 'W_top2': W_top2, 'b_top2': b_top2, 'W_top3': W_top3, 'L0_rec_W0': _L0_rec_in['W0'], 'L0_rec_b0': _L0_rec_in['b0'], 'L0_rec_W1': _L0_rec_in['W1'], 'L0_rec_b1': _L0_rec_in['b1']}

def reference(dense_ctx, ids, tbl_0, tbl_1, tbl_2, tbl_3, tbl_4, tbl_5, tbl_6, tbl_7, tbl_8, tbl_9, tbl_10, tbl_11, tbl_12, tbl_13, tbl_14, tbl_15, tbl_16, tbl_17, tbl_18, tbl_19, tbl_20, tbl_21, tbl_22, tbl_23, tbl_24, tbl_25, tbl_26, tbl_27, tbl_28, tbl_29, tbl_30, tbl_31, tbl_32, tbl_33, tbl_34, tbl_35, tbl_36, tbl_37, tbl_38, W_top1, b_top1, W_top2, b_top2, W_top3, L0_rec_W0, L0_rec_b0, L0_rec_W1, L0_rec_b1):
    import jax
    import jax.numpy as jnp

    def _L0_rec_ref(x, W0, b0, W1, b1):
        import jax, jax.numpy as jnp
        import numpy as np
        B, F, D = (512, 39, 16)
        L0, L1 = (128, 128)
        H1 = L0 // 2

        def _cin_layer(h, h0, W, b):
            z = jnp.einsum('bhd,bmd->bhmd', h, h0)
            z = z.reshape(z.shape[0], -1, z.shape[-1])
            y = jnp.einsum('oc,bcd->bod', W, z) + b[None, :, None]
            return jax.nn.relu(y)
        h0 = x
        y0 = _cin_layer(h0, h0, W0, b0)
        next_hidden, direct0 = (y0[:, :H1, :], y0[:, H1:, :])
        direct1 = _cin_layer(next_hidden, h0, W1, b1)
        result = jnp.sum(jnp.concatenate([direct0, direct1], axis=1), axis=-1)
        return result
    e = jnp.stack([tbl_0[ids[:, 0]], tbl_1[ids[:, 1]], tbl_2[ids[:, 2]], tbl_3[ids[:, 3]], tbl_4[ids[:, 4]], tbl_5[ids[:, 5]], tbl_6[ids[:, 6]], tbl_7[ids[:, 7]], tbl_8[ids[:, 8]], tbl_9[ids[:, 9]], tbl_10[ids[:, 10]], tbl_11[ids[:, 11]], tbl_12[ids[:, 12]], tbl_13[ids[:, 13]], tbl_14[ids[:, 14]], tbl_15[ids[:, 15]], tbl_16[ids[:, 16]], tbl_17[ids[:, 17]], tbl_18[ids[:, 18]], tbl_19[ids[:, 19]], tbl_20[ids[:, 20]], tbl_21[ids[:, 21]], tbl_22[ids[:, 22]], tbl_23[ids[:, 23]], tbl_24[ids[:, 24]], tbl_25[ids[:, 25]], tbl_26[ids[:, 26]], tbl_27[ids[:, 27]], tbl_28[ids[:, 28]], tbl_29[ids[:, 29]], tbl_30[ids[:, 30]], tbl_31[ids[:, 31]], tbl_32[ids[:, 32]], tbl_33[ids[:, 33]], tbl_34[ids[:, 34]], tbl_35[ids[:, 35]], tbl_36[ids[:, 36]], tbl_37[ids[:, 37]], tbl_38[ids[:, 38]]], axis=1)
    z = _L0_rec_ref(e, L0_rec_W0, L0_rec_b0, L0_rec_W1, L0_rec_b1)
    z = z.reshape(z.shape[0], -1)
    h = jnp.concatenate([z, dense_ctx], axis=1)
    h = jnp.maximum(h @ W_top1 + b_top1, 0.0)
    h = jnp.maximum(h @ W_top2 + b_top2, 0.0)
    y = h @ W_top3
    return y

_drawn_inputs = setup_inputs


def setup_inputs(seed=0):
    import zlib

    import numpy as np

    out = dict(_drawn_inputs(seed))
    spreads = {'b_top1': (0.0, 0.8),
     'b_top2': (0.0, 0.347),
     'L0_rec_b0': (0.0, 0.1),
     'L0_rec_b1': (0.0, 0.1)}
    factors = {'tbl_0': 8.0,
     'tbl_1': 8.0,
     'tbl_2': 8.0,
     'tbl_3': 8.0,
     'tbl_4': 8.0,
     'tbl_5': 8.0,
     'tbl_6': 8.0,
     'tbl_7': 8.0,
     'tbl_8': 8.0,
     'tbl_9': 8.0,
     'tbl_10': 8.0,
     'tbl_11': 8.0,
     'tbl_12': 8.0,
     'tbl_13': 8.0,
     'tbl_14': 8.0,
     'tbl_15': 8.0,
     'tbl_16': 8.0,
     'tbl_17': 8.0,
     'tbl_18': 8.0,
     'tbl_19': 8.0,
     'tbl_20': 8.0,
     'tbl_21': 8.0,
     'tbl_22': 8.0,
     'tbl_23': 8.0,
     'tbl_24': 8.0,
     'tbl_25': 8.0,
     'tbl_26': 8.0,
     'tbl_27': 8.0,
     'tbl_28': 8.0,
     'tbl_29': 8.0,
     'tbl_30': 8.0,
     'tbl_31': 8.0,
     'tbl_32': 8.0,
     'tbl_33': 8.0,
     'tbl_34': 8.0,
     'tbl_35': 8.0,
     'tbl_36': 8.0,
     'tbl_37': 8.0,
     'tbl_38': 8.0,
     'L0_rec_W0': 8.0,
     'L0_rec_W1': 3.801}
    for name, (base, spread) in spreads.items():
        noise = np.random.default_rng([zlib.crc32(name.encode()), seed]).standard_normal(out[name].shape)
        drawn = base * np.exp(spread * noise) if base else spread * noise
        out[name] = jnp.asarray(drawn.astype(out[name].dtype))
    for name, factor in factors.items():
        out[name] = (out[name] * factor).astype(out[name].dtype)
    return out
```

```python
from contextlib import ExitStack

import concourse.bass as bass
import numpy as np
from concourse import mybir

F32 = mybir.dt.float32
I32 = mybir.dt.int32
ALU = mybir.AluOpType
ACT = mybir.ActivationFunctionType
AX_X = mybir.AxisListType.X

P = 128
B, F, D = 2048, 39, 16
H1, OUT = 64, 128
TILES = B // P
HALVES = 2
DH = D // HALVES
COLS = P * DH
BANK = 512
NBANK = COLS // BANK

GROUPS = 3
P0 = GROUPS * F
SHIFT_BASE_STEP = [(0, 0), (35, 5), (4, 22), (0, 5), (28, 0)]
PAIRS = [(0, 1), (0, 3), (0, 2), (1, 2), (1, 4), (3, 4), (2, 4)]
NX = len(SHIFT_BASE_STEP)
N0 = len(PAIRS)
XROWS = max(b + s * (GROUPS - 1) for b, s in SHIFT_BASE_STEP) + F
COPIES = [(at, min(F, XROWS - at)) for at in range(0, XROWS, F)]

RY, RX, UY, VX = 4, 5, 16, 8
N1 = RY * RX

NZ = 6
REDUCE_AT = 10

HID1, HID2 = 512, 256
M1, M2 = HID1 // P, HID2 // P
QB = B // BANK

BASE = N0
PER_TILE = 2 * (N0 + N1)
AT_L0_ODD, AT_L1_EVEN, AT_L0_EVEN, AT_L1_ODD = 0, N0, N0 + N1, 2 * N0 + N1
AT_L1_LAST = N0 + N1
assert PER_TILE % NZ == 0


def interaction_kernel(nc, *, dense_t, ids, tables, w0a, w0b, b0, w1, b1, wt1, bt1, wt2, bt2, wt3, ident, out):
    with ExitStack() as ctx:
        def sb(name, shape, dt=F32):
            return ctx.enter_context(nc.sbuf_tensor(name, shape, dt))

        def ps(name, shape):
            return ctx.enter_context(nc.psum_tensor(name, shape, F32))

        def sem(name):
            return ctx.enter_context(nc.semaphore(name))

        x_dram = nc.dram_tensor("x_rows", [TILES, HALVES, XROWS, COLS], F32, kind="Internal").ap()
        y_dram = nc.dram_tensor("y_rows", [TILES, HALVES, H1, COLS], F32, kind="Internal").ap()

        ident_sb = sb("ident_sb", [P, P])
        ids_all = sb("ids_all", [P, TILES * F], I32)
        ids_now = sb("ids_now", [P, F], I32)
        emb = sb("emb", [P, F * D])
        x_stage = sb("x_stage", [F, HALVES, COLS])
        x_tiles = sb("x_tiles", [P0, NX, COLS])
        s_tiles = sb("s_tiles", [P, HALVES, RX, COLS])
        t_tiles = sb("t_tiles", [P, HALVES, RY, COLS])
        z_ring = sb("z_ring", [P, NZ, COLS])
        l0_out = sb("l0_out", [P, HALVES, COLS])
        l1_out = sb("l1_out", [P, HALVES, COLS])
        w0_sb = sb("w0_sb", [P0, N0 * OUT])
        w0b_sb = sb("w0b_sb", [P0, N0 * OUT])
        w1_sb = sb("w1_sb", [P, N1, OUT])
        b0_sb = sb("b0_sb", [P, 1])
        b1_sb = sb("b1_sb", [P, 1])
        feat_a = sb("feat_a", [P, B])
        feat_b = sb("feat_b", [P, B])
        wt1_sb = sb("wt1_sb", [P, 2, HID1])
        wt2_sb = sb("wt2_sb", [P, M1, HID2])
        wt3_sb = sb("wt3_sb", [P, M2])
        bt1_sb = sb("bt1_sb", [P, M1])
        bt2_sb = sb("bt2_sb", [P, M2])
        h1_sb = z_ring[:, 0:4, :].rearrange("p (b m) (q c) -> p b (m q) c", b=2, c=BANK)
        h2_sb = z_ring[:, 4:6, :].rearrange("p b (m c) -> p b m c", c=BANK)
        y_sb = sb("y_sb", [1, B])

        ps_x = ps("ps_x", [P, HALVES, COLS])
        ps_0 = ps("ps_0", [P, COLS])
        ps_1 = ps("ps_1", [P, COLS])

        consts_in = sem("consts_in")
        ids_in = sem("ids_in")
        ids_copied = sem("ids_copied")
        gathered = sem("gathered")
        gather_begun = sem("gather_begun")
        transpose_begun = sem("transpose_begun")
        w0_summed = sem("w0_summed")
        feat_zeroed = sem("feat_zeroed")
        dense_in = sem("dense_in")
        x_transposed = sem("x_transposed")
        x_staged = sem("x_staged")
        x_written = [sem(f"x_written{h}") for h in range(HALVES)]
        x_loaded = [sem(f"x_loaded{j}") for j in range(NX)]
        s_loaded = [[sem(f"s_loaded{h}_{k}") for k in range(RX)] for h in range(HALVES)]
        t_loaded = [[sem(f"t_loaded{h}_{j}") for j in range(RY)] for h in range(HALVES)]
        y_written = [sem(f"y_written{h}") for h in range(HALVES)]
        products_formed = sem("products_formed")
        products_used = sem("products_used")
        l0_evacuated = sem("l0_evacuated")
        l1_evacuated = sem("l1_evacuated")
        reduced0 = sem("reduced0")
        reduced1 = sem("reduced1")
        h1_summed = sem("h1_summed")
        h1_ready = sem("h1_ready")
        h2_summed = sem("h2_summed")
        h2_ready = sem("h2_ready")
        y_summed = sem("y_summed")
        y_ready = sem("y_ready")
        y_out = sem("y_out")
        CONSTS = 11
        head_banks = [acc[:, q * BANK:(q + 1) * BANK] for acc in (ps_0, ps_1, ps_x[:, 0, :], ps_x[:, 1, :]) for q in range(2)]

        block = ctx.enter_context(nc.Block())

        def x_view(i, h, j):
            base, step = SHIFT_BASE_STEP[j]
            rows = x_dram[i, h]
            return bass.AP(rows.tensor, rows.offset + base * COLS, [[COLS, F], [step * COLS, GROUPS], [1, COLS]])

        def s_view(i, h, k):
            rows = x_dram[i, h]
            return bass.AP(rows.tensor, rows.offset + k * COLS, [[0, UY], [RX * COLS, VX], [1, COLS]])

        def t_view(i, h, j):
            rows = y_dram[i, h]
            return bass.AP(rows.tensor, rows.offset + j * COLS, [[RY * COLS, UY], [0, VX], [1, COLS]])

        @block.sync
        def _(sp):
            sp.dma_start(ids_all[:], ids).then_inc(ids_in, 16)
            for dst, src in ((ident_sb, ident), (w0_sb, w0a), (w0b_sb, w0b), (b0_sb, b0), (w1_sb, w1), (b1_sb, b1),
                             (wt1_sb, wt1), (wt2_sb, wt2), (wt3_sb, wt3), (bt1_sb, bt1), (bt2_sb, bt2)):
                sp.dma_start(dst[:], src).then_inc(consts_in, 16)
            sp.wait_ge(feat_zeroed, 1)
            sp.dma_start(feat_b[0:D, :], dense_t).then_inc(dense_in, 16)

            def write_x(i):
                for h in range(HALVES):
                    sp.wait_ge(x_staged, 2 * i + h + 1)
                    for at, count in COPIES:
                        sp.dma_start(x_dram[i, h, at:at + count], x_stage[0:count, h, :]).then_inc(x_written[h], 16)

            def load_x(i, h):
                sp.wait_ge(x_written[h], 16 * len(COPIES) * (i + 1))
                for j in range(NX):
                    sp.dma_start(x_tiles[:, j, :], x_view(i, h, j)).then_inc(x_loaded[j], 16)

            def load_s(i, h, free_from=None):
                for k in range(RX):
                    if free_from is not None:
                        sp.wait_ge(products_formed, free_from + RY * (k + 1))
                    sp.dma_start(s_tiles[:, h, k, :], s_view(i, h, k)).then_inc(s_loaded[h][k], 16)

            def write_y(i, h):
                sp.wait_ge(l0_evacuated, 2 * i + h + 1)
                sp.dma_start(y_dram[i, h], l0_out[0:H1, h, :]).then_inc(y_written[h], 16)

            def load_t(i, h):
                sp.wait_ge(y_written[h], 16 * (i + 1))
                for j in range(RY):
                    sp.dma_start(t_tiles[:, h, j, :], t_view(i, h, j)).then_inc(t_loaded[h][j], 16)

            write_x(0)
            load_x(0, 0)
            load_s(0, 0)
            sp.wait_ge(products_formed, BASE)
            load_x(0, 1)
            load_s(0, 1)
            write_y(0, 0)
            load_t(0, 0)
            write_y(0, 1)
            load_t(0, 1)
            with sp.Fori(0, TILES - 1) as i:
                base = i * PER_TILE + BASE
                write_x(i + 1)
                sp.wait_ge(products_formed, base + AT_L1_EVEN)
                load_x(i + 1, 0)
                load_s(i + 1, 0, base + AT_L1_EVEN)
                write_y(i + 1, 0)
                load_t(i + 1, 0)
                sp.wait_ge(products_formed, base + AT_L1_ODD)
                load_x(i + 1, 1)
                load_s(i + 1, 1, base + AT_L1_ODD)
                write_y(i + 1, 1)
                load_t(i + 1, 1)
            sp.wait_ge(y_ready, QB)
            sp.dma_start(out.rearrange("b o -> o b"), y_sb[:]).then_inc(y_out, 16)
            sp.wait_ge(y_out, 16)

        @block.gpsimd
        def _(pool):
            def gather(i):
                nc.gpsimd.tensor_copy(ids_now[:], ids_all[:, bass.ds(i * F, F)]).then_inc(ids_copied, 1)
                pool.wait_ge(ids_copied, i + 1)
                pool.sem_inc(gather_begun, 1)
                for f in range(F):
                    nc.gpsimd.indirect_dma_start(
                        out=emb[:, f * D:(f + 1) * D], out_offset=None, in_=tables[f],
                        in_offset=bass.IndirectOffsetOnAxis(ap=ids_now[:, f:f + 1], axis=0),
                    ).then_inc(gathered, 16)

            pool.wait_ge(ids_in, 16)
            gather(0)
            with pool.Fori(1, TILES) as i:
                pool.wait_ge(gathered, i * (16 * F))
                pool.wait_ge(x_transposed, i * HALVES)
                gather(i)

        @block.tensor
        def _(pe):
            emb_v = emb[:].rearrange("p (f d) -> p f d", d=D)

            def transpose_x(i):
                pe.wait_ge(gathered, (i + 1) * (16 * F))
                pe.sem_inc(transpose_begun, 1)
                for h in range(HALVES):
                    for d in range(DH):
                        last = nc.tensor.transpose(ps_x[0:F, h, d * P:(d + 1) * P], emb_v[:, :, h * DH + d],
                                                   ident_sb[:])
                    last.then_inc(x_transposed, 1)

            def products(acc, weights, rows, start, count, slot):
                for n in range(count):
                    pe.wait_ge(products_formed, start + (n + 1))
                    for q in range(COLS // BANK):
                        cols = slice(q * BANK, (q + 1) * BANK)
                        last = nc.tensor.matmul(acc[:, cols], weights(n), z_ring[0:rows, (slot + n) % NZ, cols],
                                                start=(n == 0), stop=(n == count - 1))
                    last.then_inc(products_used, 1)

            def layer0(start, slot):
                products(ps_0, lambda n: w0_sb[:, n * OUT:(n + 1) * OUT], P0, start, N0, slot)

            def layer1(start, slot):
                products(ps_1, lambda n: w1_sb[:, n, :], P, start, N1, slot)

            pe.wait_ge(consts_in, 16 * CONSTS)
            transpose_x(0)
            pe.wait_ge(w0_summed, 1)
            layer0(0, 0)
            with pe.Fori(0, TILES - 1) as i:
                base = i * PER_TILE + BASE
                pe.wait_ge(x_staged, (i + 1) * HALVES)
                transpose_x(i + 1)
                pe.wait_ge(l0_evacuated, i * HALVES + 1)
                layer0(base + AT_L0_ODD, BASE + AT_L0_ODD)
                pe.wait_ge(l1_evacuated, i * HALVES + 1)
                layer1(base + AT_L1_EVEN, BASE + AT_L1_EVEN)
                pe.wait_ge(l0_evacuated, i * HALVES + 2)
                layer0(base + AT_L0_EVEN, BASE + AT_L0_EVEN)
                pe.wait_ge(l1_evacuated, i * HALVES + 2)
                layer1(base + AT_L1_ODD, BASE + AT_L1_ODD)
            i = TILES - 1
            base = i * PER_TILE + BASE
            pe.wait_ge(l0_evacuated, i * HALVES + 1)
            layer0(base + AT_L0_ODD, BASE + AT_L0_ODD)
            pe.wait_ge(l1_evacuated, i * HALVES + 1)
            layer1(base + AT_L1_EVEN, BASE + AT_L1_EVEN)
            pe.wait_ge(l1_evacuated, i * HALVES + 2)
            layer1(base + AT_L1_LAST, BASE + AT_L1_LAST)

            def head1(q):
                cols = slice(q * BANK, (q + 1) * BANK)
                for m in range(M1):
                    if q > 0:
                        pe.wait_ge(h1_ready, M1 * (q - 1) + m + 1)
                    for kt, feat in enumerate((feat_a, feat_b)):
                        last = nc.tensor.matmul(head_banks[m], wt1_sb[:, kt, m * P:(m + 1) * P], feat[:, cols],
                                                start=(kt == 0), stop=(kt == 1))
                    last.then_inc(h1_summed, 1)

            def head2(q):
                pe.wait_ge(h1_ready, M1 * (q + 1))
                for m in range(M2):
                    if q > 0:
                        pe.wait_ge(h2_ready, M2 * (q - 1) + m + 1)
                    for kt in range(M1):
                        last = nc.tensor.matmul(head_banks[M1 + m], wt2_sb[:, kt, m * P:(m + 1) * P],
                                                h1_sb[:, q % 2, kt, :], start=(kt == 0), stop=(kt == M1 - 1))
                    last.then_inc(h2_summed, 1)

            def head3(q):
                pe.wait_ge(h2_ready, M2 * (q + 1))
                if q > 0:
                    pe.wait_ge(y_ready, q)
                for kt in range(M2):
                    last = nc.tensor.matmul(head_banks[M1 + M2][0:1, :], wt3_sb[:, kt:kt + 1],
                                            h2_sb[:, q % 2, kt, :], start=(kt == 0), stop=(kt == M2 - 1))
                last.then_inc(y_summed, 1)

            pe.wait_ge(dense_in, 16)
            pe.wait_ge(reduced0, TILES)
            pe.wait_ge(reduced1, TILES)
            pe.wait_ge(l0_evacuated, TILES * HALVES)
            pe.wait_ge(l1_evacuated, TILES * HALVES + 1)
            pe.wait_ge(x_staged, TILES * HALVES)
            for q in range(QB + 2):
                if q < QB:
                    head1(q)
                if 1 <= q <= QB:
                    head2(q - 1)
                if q >= 2:
                    head3(q - 2)

        @block.scalar
        def _(act):
            def stage_x(i):
                for h in range(HALVES):
                    act.wait_ge(x_transposed, i * HALVES + h + 1)
                    nc.scalar.activation(x_stage[:, h, :], ps_x[0:F, h, :], ACT.Copy).then_inc(x_staged, 1)

            def evacuate0(h, used):
                act.wait_ge(products_used, used)
                nc.scalar.activation(l0_out[:, h, :], ps_0[:], ACT.Relu, bias=b0_sb[:]).then_inc(l0_evacuated, 1)

            def evacuate1(h, used):
                act.wait_ge(products_used, used)
                nc.scalar.activation(l1_out[:, h, :], ps_1[:], ACT.Relu, bias=b1_sb[:]).then_inc(l1_evacuated, 1)

            act.sem_inc(l1_evacuated, 1)
            act.wait_ge(consts_in, 16 * CONSTS)
            stage_x(0)
            evacuate0(0, BASE)
            with act.Fori(0, TILES - 1) as i:
                base = i * PER_TILE + BASE
                for h in range(HALVES):
                    act.wait_ge(x_written[h], (i + 1) * (16 * len(COPIES)))
                stage_x(i + 1)
                evacuate0(1, base + AT_L0_ODD + N0)
                evacuate1(0, base + AT_L1_EVEN + N1)
                act.wait_ge(y_written[0], (i + 1) * 16)
                act.wait_ge(reduced0, i + 1)
                evacuate0(0, base + AT_L0_EVEN + N0)
                evacuate1(1, base + AT_L1_ODD + N1)
                act.wait_ge(y_written[1], (i + 1) * 16)
                act.wait_ge(reduced1, i + 1)
            i = TILES - 1
            base = i * PER_TILE + BASE
            evacuate0(1, base + AT_L0_ODD + N0)
            evacuate1(0, base + AT_L1_EVEN + N1)
            evacuate1(1, base + AT_L1_LAST + N1)

            def take1(q):
                if q >= 2:
                    act.wait_ge(h2_summed, M2 * (q - 1))
                for m in range(M1):
                    act.wait_ge(h1_summed, M1 * q + m + 1)
                    nc.scalar.activation(h1_sb[:, q % 2, m, :], head_banks[m], ACT.Relu,
                                         bias=bt1_sb[:, m:m + 1]).then_inc(h1_ready, 1)

            def take2(q):
                if q >= 2:
                    act.wait_ge(y_summed, q - 1)
                for m in range(M2):
                    act.wait_ge(h2_summed, M2 * q + m + 1)
                    nc.scalar.activation(h2_sb[:, q % 2, m, :], head_banks[M1 + m], ACT.Relu,
                                         bias=bt2_sb[:, m:m + 1]).then_inc(h2_ready, 1)

            for q in range(QB + 1):
                if q < QB:
                    take1(q)
                if q >= 1:
                    take2(q - 1)

        @block.vector
        def _(dve):
            def layer0(start, slot, i, h):
                ready = set()
                for n, (a, b) in enumerate(PAIRS):
                    for j in (a, b):
                        if j not in ready:
                            dve.wait_ge(x_loaded[j], (i * HALVES + h + 1) * 16)
                            ready.add(j)
                    form(z_ring[0:P0, (slot + n) % NZ, :], x_tiles[:, a, :], x_tiles[:, b, :], start, n)

            def form(z, a, b, start, n):
                if not isinstance(start, int) or start + n >= NZ:
                    dve.wait_ge(products_used, start + (n + 1 - NZ))
                nc.vector.tensor_tensor(z, a, b, ALU.mult).then_inc(products_formed, 1)

            def layer1(start, slot, i, h, reductions=()):
                for n in range(N1):
                    k, j = divmod(n, RY)
                    if j == 0:
                        dve.wait_ge(s_loaded[h][k], (i + 1) * 16)
                    if k == 0:
                        dve.wait_ge(t_loaded[h][j], (i + 1) * 16)
                    form(z_ring[:, (slot + n) % NZ, :], s_tiles[:, h, k, :], t_tiles[:, h, j, :], start, n)
                    if n == REDUCE_AT:
                        for reduce in reductions:
                            reduce()

            def reduce0(i):
                dve.wait_ge(l0_evacuated, (i + 1) * HALVES)
                rows = l0_out[H1:P, :, :].rearrange("p h (d b) -> p b (h d)", b=P)
                nc.vector.tensor_reduce(feat_b[H1:P, bass.ds(i * P, P)], rows, AX_X, ALU.add).then_inc(reduced0, 1)

            def reduce1(i):
                dve.wait_ge(l1_evacuated, (i + 1) * HALVES + 1)
                rows = l1_out[:].rearrange("p h (d b) -> p b (h d)", b=P)
                nc.vector.tensor_reduce(feat_a[:, bass.ds(i * P, P)], rows, AX_X, ALU.add).then_inc(reduced1, 1)

            def batch_tile(i, reductions):
                base = i * PER_TILE + BASE
                layer0(base + AT_L0_ODD, BASE + AT_L0_ODD, i, 1)
                layer1(base + AT_L1_EVEN, BASE + AT_L1_EVEN, i, 0, reductions)
                layer0(base + AT_L0_EVEN, BASE + AT_L0_EVEN, i + 1, 0)
                layer1(base + AT_L1_ODD, BASE + AT_L1_ODD, i, 1)

            nc.vector.memset(feat_b[0:H1, :], 0.0).then_inc(feat_zeroed, 1)
            dve.wait_ge(consts_in, 16 * CONSTS)
            nc.vector.tensor_tensor(w0_sb[:], w0_sb[:], w0b_sb[:], ALU.add).then_inc(w0_summed, 1)
            layer0(0, 0, 0, 0)
            batch_tile(0, [lambda: reduce0(0)])
            with dve.Fori(1, TILES - 1) as i:
                batch_tile(i, [lambda: reduce1(i - 1), lambda: reduce0(i)])
            i = TILES - 1
            base = i * PER_TILE + BASE
            layer0(base + AT_L0_ODD, BASE + AT_L0_ODD, i, 1)
            layer1(base + AT_L1_EVEN, BASE + AT_L1_EVEN, i, 0, [lambda: reduce1(i - 1), lambda: reduce0(i)])
            layer1(base + AT_L1_LAST, BASE + AT_L1_LAST, i, 1)
            reduce1(i)
            for q in range(QB):
                dve.wait_ge(y_summed, q + 1)
                nc.vector.tensor_copy(y_sb[:, q * BANK:(q + 1) * BANK],
                                      head_banks[M1 + M2][0:1, :]).then_inc(y_ready, 1)


def shifts(j, r):
    base, step = SHIFT_BASE_STEP[j]
    return [(r + base + step * g) % F for g in range(GROUPS)]


def layer0_rows():
    forward = np.full((P0, N0), -1)
    backward = np.full((P0, N0), -1)
    seen = set()
    for n, (a, b) in enumerate(PAIRS):
        for r in range(F):
            for g, (h, m) in enumerate(zip(shifts(a, r), shifts(b, r))):
                if (min(h, m), max(h, m)) in seen:
                    continue
                seen.add((min(h, m), max(h, m)))
                forward[r * GROUPS + g, n] = h * F + m
                if h != m:
                    backward[r * GROUPS + g, n] = m * F + h
    assert len(seen) == F * (F + 1) // 2
    return forward, backward


def layer1_rows():
    place = np.full((P, N1), -1)
    for p in range(P):
        u, v = divmod(p, VX)
        for n in range(N1):
            k, j = divmod(n, RY)
            if RX * v + k < F:
                place[p, n] = (RY * u + j) * F + RX * v + k
    return place


def rows_or_zero(w, place):
    laid = np.zeros(place.shape + (w.shape[0],), w.dtype)
    laid[place >= 0] = w.T[place[place >= 0]]
    return laid


def kernel(**inputs):
    import concourse.bacc as bacc
    from concourse.bass_utils import run_bass_kernel_spmd

    a = {name: np.asarray(x) for name, x in inputs.items()}
    forward, backward = layer0_rows()
    w_top1 = np.zeros((P, 2, HID1), a["W_top1"].dtype)
    w_top1[:, 0] = a["W_top1"][H1:H1 + OUT]
    w_top1[0:D, 1] = a["W_top1"][H1 + OUT:]
    w_top1[H1:, 1] = a["W_top1"][0:H1]
    arrays = {
        "dense_t": a["dense_ctx"].T,
        "ids": a["ids"].reshape(TILES, P, F).transpose(1, 0, 2).reshape(P, TILES * F),
        "w0a": rows_or_zero(a["L0_rec_W0"], forward).reshape(P0, N0 * OUT),
        "w0b": rows_or_zero(a["L0_rec_W0"], backward).reshape(P0, N0 * OUT),
        "b0": a["L0_rec_b0"].reshape(P, 1),
        "w1": rows_or_zero(a["L0_rec_W1"], layer1_rows()),
        "b1": a["L0_rec_b1"].reshape(P, 1),
        "wt1": w_top1,
        "bt1": a["b_top1"].reshape(M1, P).T,
        "wt2": a["W_top2"].reshape(M1, P, HID2).transpose(1, 0, 2),
        "bt2": a["b_top2"].reshape(M2, P).T,
        "wt3": a["W_top3"].reshape(M2, P).T,
        "ident": np.eye(P, dtype=np.float32),
    }
    arrays |= {f"tbl_{f}": a[f"tbl_{f}"] for f in range(F)}
    arrays = {f"in_{name}": np.ascontiguousarray(x) for name, x in arrays.items()}
    nc = bacc.Bacc("TRN2", target_bir_lowering=False, num_devices=1)
    aps = {name: nc.dram_tensor(name, x.shape, mybir.dt.from_np(x.dtype), kind="ExternalInput").ap()
           for name, x in arrays.items()}
    out = nc.dram_tensor("out_y", (B, 1), F32, kind="ExternalOutput").ap()
    names = ("dense_t", "ids", "w0a", "w0b", "b0", "w1", "b1", "wt1", "bt1", "wt2", "bt2", "wt3", "ident")
    interaction_kernel(nc, tables=[aps[f"in_tbl_{f}"] for f in range(F)], out=out,
                       **{name: aps[f"in_{name}"] for name in names})
    result = run_bass_kernel_spmd(nc, [arrays], core_ids=[0])
    return result.results[0]["out_y"]
```

```python
from collections import namedtuple
from contextlib import ExitStack

import concourse.bass as bass
import numpy as np
from concourse import mybir

F32 = mybir.dt.float32
F32R = mybir.dt.float32r
I32 = mybir.dt.int32
ALU = mybir.AluOpType
ACT = mybir.ActivationFunctionType
AX_X = mybir.AxisListType.X

P = 128
B, F, D = 2048, 39, 16
H1, OUT = 64, 128
TILES = B // P
HALVES = 2
DH = D // HALVES
COLS = P * DH
BANK = 512
NBANK = COLS // BANK

GROUPS = 3
P0 = GROUPS * F
SHIFT_BASE_STEP = [(0, 0), (35, 5), (4, 22), (0, 5), (28, 0)]
NX = len(SHIFT_BASE_STEP)
XROWS = max(b + s * (GROUPS - 1) for b, s in SHIFT_BASE_STEP) + F
COPIES = [(at, min(F, XROWS - at)) for at in range(0, XROWS, F)]

RY, RX, UY, VX = 4, 5, 16, 8

UNITS0 = [[(0, 2), (1, 2)], [(1, 4), (2, 4)], [(3, 4)], [(0, 1), (0, 3)]]
UNITS1 = [[(k, j), (k, j + 1)] for k in range(RX) for j in range(0, RY, 2)]
SPLIT_AT0, SPLIT_AT1 = (2,), (1, 3, 6, 8)


def steps_of(units, split_at):
    return [(units[n - 1] if n - 1 in split_at else None, unit)
            for n, unit in enumerate(units) if n not in split_at]


STEPS0, STEPS1 = steps_of(UNITS0, SPLIT_AT0), steps_of(UNITS1, SPLIT_AT1)
REDUCE_AT = 1
NPLAIN, NSPLIT = 3, 2
AHEAD = 1

HID1, HID2 = 512, 256
M1, M2 = HID1 // P, HID2 // P
QB = B // BANK
TILES_PER_Q = TILES // QB

Count = namedtuple("Count", "units plains splits")


def size(steps):
    splits = sum(split is not None for split, _ in steps)
    return Count(len(steps) + splits, len(steps), splits)


def plus(*counts):
    return Count(*(sum(column) for column in zip(*counts)))


def split_units(steps):
    found, formed = [], 0
    for split, _ in steps:
        if split is not None:
            found.append((formed + 1, split))
        formed += 1 if split is None else 2
    return found


C0, C1 = size(STEPS0), size(STEPS1)
PROLOGUE = Count(0, 0, 0)
L0_ODD = C0
L1_EVEN = plus(C0, C0)
L0_EVEN = L1_LAST = plus(C0, C0, C1)
L1_ODD = plus(C0, C0, C1, C0)
PER_TILE = plus(C0, C0, C1, C1)
assert PER_TILE.plains % NPLAIN == 0 and PER_TILE.splits % NSPLIT == 0


def before(i, turn):
    return Count(*(i * per + at for per, at in zip(PER_TILE, turn)))


def products_of(steps, split):
    return sorted(pair for step in steps for pair in (step[0] if split else step[1]) or ())


PLAIN0, SPLIT0 = products_of(STEPS0, False), products_of(STEPS0, True)
PLAIN1, SPLIT1 = products_of(STEPS1, False), products_of(STEPS1, True)


def interaction_kernel(nc, *, dense_t, ids, tables, w0_plain, w0_split, b0, w1_plain, w1_split, b1,
                       wt1, bt1, wt2, bt2, wt3, ident, out):
    with ExitStack() as ctx:
        def sb(name, shape, dt=F32):
            return ctx.enter_context(nc.sbuf_tensor(name, shape, dt))

        def ps(name, shape):
            return ctx.enter_context(nc.psum_tensor(name, shape, F32))

        def sem(name):
            return ctx.enter_context(nc.semaphore(name))

        x_dram = nc.dram_tensor("x_rows", [TILES, HALVES, XROWS, COLS], F32, kind="Internal").ap()
        y_dram = nc.dram_tensor("y_rows", [TILES, HALVES, H1, COLS], F32, kind="Internal").ap()

        ident_sb = sb("ident_sb", [P, P])
        ids_now = sb("ids_now", [P, F], I32)
        emb = sb("emb", [P, F * D])
        x_stage = sb("x_stage", [P, COLS])
        x_tiles = sb("x_tiles", [P0, NX, COLS])
        s_tiles = sb("s_tiles", [P, HALVES, RX, COLS])
        t_tiles = sb("t_tiles", [P, HALVES, RY, COLS])
        plain_ring = sb("plain_ring", [P, NPLAIN, 2, COLS])
        split_whole = sb("split_whole", [P, 2, COLS])
        high_ring = sb("high_ring", [P, NSPLIT, 2, COLS], F32R)
        low_ring = sb("low_ring", [P, NSPLIT, 2, COLS], F32R)
        l0_out = sb("l0_out", [P, DH + 1, P])
        l1_out = sb("l1_out", [P, DH + 1, P])
        l0_cols = l0_out[:, 0:DH, :].rearrange("p d b -> p (d b)")
        l1_cols = l1_out[:, 0:DH, :].rearrange("p d b -> p (d b)")
        w0_sb = sb("w0_sb", [P0, len(PLAIN0), OUT])
        w0_high = sb("w0_high", [P0, len(SPLIT0), OUT], F32R)
        w0_low = sb("w0_low", [P0, len(SPLIT0), OUT], F32R)
        w1_sb = sb("w1_sb", [P, len(PLAIN1), OUT])
        w1_high = sb("w1_high", [P, len(SPLIT1), OUT], F32R)
        w1_low = sb("w1_low", [P, len(SPLIT1), OUT], F32R)
        b0_sb = sb("b0_sb", [P, 1])
        b1_sb = sb("b1_sb", [P, 1])
        feat_a = sb("feat_a", [P, B])
        feat_b = sb("feat_b", [P, B])
        wt3_sb = sb("wt3_sb", [P, M2])
        bt1_sb = sb("bt1_sb", [P, M1])
        bt2_sb = sb("bt2_sb", [P, M2])

        w0_plain_in = plain_ring[0:P0, 0, :, :].rearrange("p a c -> p (a c)")[:, 0:2 * len(PLAIN0) * OUT]
        w0_plain_in = w0_plain_in.rearrange("p (o n c) -> p o n c", o=2, c=OUT)
        w0_split_in = plain_ring[0:P0, 1, :, :].rearrange("p a c -> p (a c)")[:, 0:2 * len(SPLIT0) * OUT]
        w0_split_in = w0_split_in.rearrange("p (o n c) -> p o n c", o=2, c=OUT)
        w1_split_in = l1_cols[:, 0:len(SPLIT1) * OUT]
        w1_split_in = w1_split_in.rearrange("p (n c) -> p n c", c=OUT)

        wt1_sb = s_tiles[:, 0, 0, :].rearrange("p (a c) -> p a c", c=HID1)
        wt2_sb = s_tiles[:, 0, 1, :].rearrange("p (a c) -> p a c", c=HID2)
        h1_sb = plain_ring[:, 0:2].rearrange("p b m (q c) -> p b (m q) c", c=BANK)
        h2_sb = split_whole[:].rearrange("p b (m c) -> p b m c", c=BANK)
        y_sb = feat_b[0:1, :]

        ps_x = ps("ps_x", [P, HALVES, COLS])
        ps_0 = ps("ps_0", [P, COLS])
        ps_1 = ps("ps_1", [P, COLS])
        head_banks = [acc[:, q * BANK:(q + 1) * BANK]
                      for acc in (ps_x[:, 0, :], ps_x[:, 1, :], ps_0, ps_1) for q in range(2)]

        consts_in = sem("consts_in")
        ids_in = sem("ids_in")
        gathered = sem("gathered")
        gather_begun = sem("gather_begun")
        transpose_begun = sem("transpose_begun")
        weights_summed = sem("weights_summed")
        weights_high = sem("weights_high")
        weights_split = sem("weights_split")
        feat_zeroed = sem("feat_zeroed")
        dense_in = sem("dense_in")
        x_transposed = sem("x_transposed")
        x_staged = sem("x_staged")
        x_written = [sem(f"x_written{h}") for h in range(HALVES)]
        x_loaded = [sem(f"x_loaded{j}") for j in range(NX)]
        s_loaded = [[sem(f"s_loaded{h}_{k}") for k in range(RX)] for h in range(HALVES)]
        t_loaded = [[sem(f"t_loaded{h}_{j}") for j in range(RY)] for h in range(HALVES)]
        y_written = [sem(f"y_written{h}") for h in range(HALVES)]
        units_formed = sem("units_formed")
        highs_formed = sem("highs_formed")
        lows_formed = sem("lows_formed")
        plains_used = sem("plains_used")
        splits_used = sem("splits_used")
        l0_evacuated = sem("l0_evacuated")
        l1_evacuated = sem("l1_evacuated")
        reduced0 = sem("reduced0")
        reduced1 = sem("reduced1")
        head_weights_in = sem("head_weights_in")
        h1_summed = sem("h1_summed")
        h1_ready = sem("h1_ready")
        h2_summed = sem("h2_summed")
        h2_ready = sem("h2_ready")
        y_summed = sem("y_summed")
        y_ready = sem("y_ready")
        y_out = sem("y_out")

        consts = ((ident_sb, ident), (w0_plain_in, w0_plain), (w0_split_in, w0_split), (b0_sb, b0),
                  (w1_split_in, w1_split), (w1_sb, w1_plain), (b1_sb, b1), (wt3_sb, wt3), (bt1_sb, bt1),
                  (bt2_sb, bt2))
        CONSTS_LANDED = 16 * len(consts)

        block = ctx.enter_context(nc.Block())

        def x_view(i, h, j):
            base, step = SHIFT_BASE_STEP[j]
            rows = x_dram[i, h]
            return bass.AP(rows.tensor, rows.offset + base * COLS, [[COLS, F], [step * COLS, GROUPS], [1, COLS]])

        def s_view(i, h, k):
            rows = x_dram[i, h]
            return bass.AP(rows.tensor, rows.offset + k * COLS, [[0, UY], [RX * COLS, VX], [1, COLS]])

        def t_view(i, h, j):
            rows = y_dram[i, h]
            return bass.AP(rows.tensor, rows.offset + j * COLS, [[RY * COLS, UY], [0, VX], [1, COLS]])

        @block.sync
        def _(sp):
            for dst, src in consts:
                sp.dma_start(dst[:], src).then_inc(consts_in, 16)
            sp.wait_ge(feat_zeroed, 1)
            sp.dma_start(feat_b[0:D, :], dense_t).then_inc(dense_in, 16)

            def write_x(i):
                for h in range(HALVES):
                    sp.wait_ge(x_staged, 2 * i + h + 1)
                    for at, count in COPIES:
                        sp.dma_start(x_dram[i, h, at:at + count], x_stage[h * 64:h * 64 + count, :])\
                            .then_inc(x_written[h], 16)

            def load_x(i, h):
                sp.wait_ge(x_written[h], 16 * len(COPIES) * (i + 1))
                for j in (2, 0, 1, 4, 3):
                    sp.dma_start(x_tiles[:, j, :], x_view(i, h, j)).then_inc(x_loaded[j], 16)

            def load_s(i, h, turn=None):
                for k in range(RX):
                    if turn is not None:
                        sp.wait_ge(units_formed, turn.units + 2 * (k + 1))
                    sp.dma_start(s_tiles[:, h, k, :], s_view(i, h, k)).then_inc(s_loaded[h][k], 16)

            def write_y(i, h):
                sp.wait_ge(l0_evacuated, 2 * i + h + 1)
                sp.dma_start(y_dram[i, h], l0_cols[0:H1, :]).then_inc(y_written[h], 16)

            def load_t(i, h):
                sp.wait_ge(y_written[h], 16 * (i + 1))
                for j in range(RY):
                    sp.dma_start(t_tiles[:, h, j, :], t_view(i, h, j)).then_inc(t_loaded[h][j], 16)

            write_x(0)
            load_x(0, 0)
            load_s(0, 0)
            sp.wait_ge(units_formed, C0.units)
            load_x(0, 1)
            write_y(0, 0)
            load_t(0, 0)
            load_s(0, 1)
            write_y(0, 1)
            load_t(0, 1)
            with sp.Fori(0, TILES - 1) as i:
                write_x(i + 1)
                sp.wait_ge(units_formed, before(i, L1_EVEN).units)
                load_x(i + 1, 0)
                load_s(i + 1, 0, before(i, L1_EVEN))
                write_y(i + 1, 0)
                load_t(i + 1, 0)
                sp.wait_ge(units_formed, before(i, L1_ODD).units)
                load_x(i + 1, 1)
                load_s(i + 1, 1, before(i, L1_ODD))
                write_y(i + 1, 1)
                load_t(i + 1, 1)
            sp.wait_ge(units_formed, before(TILES - 1, L1_LAST).units)
            sp.dma_start(wt1_sb, wt1).then_inc(head_weights_in, 16)
            sp.dma_start(wt2_sb, wt2).then_inc(head_weights_in, 16)
            sp.wait_ge(y_ready, QB)
            sp.dma_start(out.rearrange("b o -> o b"), y_sb).then_inc(y_out, 16)
            sp.wait_ge(y_out, 16)

        @block.gpsimd
        def _(pool):
            def gather(i):
                pool.dma_start(ids_now[:], ids[i]).then_inc(ids_in, 16)
                pool.wait_ge(ids_in, (i + 1) * 16)
                pool.sem_inc(gather_begun, 1)
                for f in range(F):
                    nc.gpsimd.indirect_dma_start(
                        out=emb[:, f * D:(f + 1) * D], out_offset=None, in_=tables[f],
                        in_offset=bass.IndirectOffsetOnAxis(ap=ids_now[:, f:f + 1], axis=0),
                    ).then_inc(gathered, 16)

            gather(0)
            with pool.Fori(1, TILES) as i:
                pool.wait_ge(gathered, i * (16 * F))
                pool.wait_ge(x_transposed, i * HALVES)
                gather(i)

        @block.tensor
        def _(pe):
            emb_v = emb[:].rearrange("p (f d) -> p f d", d=D)

            def transpose_x(i):
                pe.wait_ge(gathered, (i + 1) * (16 * F))
                pe.sem_inc(transpose_begun, 1)
                for h in range(HALVES):
                    for d in range(DH):
                        last = nc.tensor.transpose(ps_x[0:F, h, d * P:(d + 1) * P], emb_v[:, :, h * DH + d],
                                                   ident_sb[:])
                    last.then_inc(x_transposed, 1)

            def plain(acc, unit, weights, order, slot, rows, first, last):
                for n, pair in enumerate(unit):
                    for q in range(COLS // BANK):
                        cols = slice(q * BANK, (q + 1) * BANK)
                        mm = nc.tensor.matmul(acc[:, cols], weights[:, order.index(pair), :],
                                              plain_ring[0:rows, slot, n, cols],
                                              start=(first and n == 0), stop=(last and n == len(unit) - 1))
                mm.then_inc(plains_used, 1)

            def split(acc, unit, high, low, order, slot, rows, last):
                for n, pair in enumerate(unit):
                    passes = ((high, high_ring), (low, high_ring), (high, low_ring))
                    for m, (weights, ring) in enumerate(passes):
                        for q in range(COLS // BANK):
                            cols = slice(q * BANK, (q + 1) * BANK)
                            mm = nc.tensor.matmul(acc[:, cols], weights[:, order.index(pair), :],
                                                  ring[0:rows, slot, n, cols], start=False,
                                                  stop=(last and n == len(unit) - 1 and m == 2))
                mm.then_inc(splits_used, 1)

            def layer(acc, steps, rows, weights, orders, done, turn):
                whole, high, low = weights
                plains = splits = units = 0
                for step, (split_unit, plain_unit) in enumerate(steps):
                    end = step == len(steps) - 1
                    units += 1 if split_unit is None else 2
                    pe.wait_ge(units_formed, done.units + units)
                    plain(acc, plain_unit, whole, orders[0], (turn.plains + plains) % NPLAIN, rows,
                          step == 0, end and split_unit is None)
                    plains += 1
                    if split_unit is not None:
                        pe.wait_ge(lows_formed, done.splits + (splits + 1))
                        split(acc, split_unit, high, low, orders[1], (turn.splits + splits) % NSPLIT, rows, end)
                        splits += 1

            def layer0(i, turn):
                layer(ps_0, STEPS0, P0, (w0_sb, w0_high, w0_low), (PLAIN0, SPLIT0), before(i, turn), turn)

            def layer1(i, turn):
                layer(ps_1, STEPS1, P, (w1_sb, w1_high, w1_low), (PLAIN1, SPLIT1), before(i, turn), turn)

            pe.wait_ge(consts_in, CONSTS_LANDED)
            transpose_x(0)
            pe.wait_ge(weights_split, 2)
            layer0(0, PROLOGUE)
            with pe.Fori(0, TILES - 1) as i:
                pe.wait_ge(l0_evacuated, i * HALVES + 1)
                layer0(i, L0_ODD)
                pe.wait_ge(x_staged, (i + 1) * HALVES)
                transpose_x(i + 1)
                pe.wait_ge(l1_evacuated, i * HALVES + 1)
                layer1(i, L1_EVEN)
                pe.wait_ge(l0_evacuated, i * HALVES + 2)
                layer0(i, L0_EVEN)
                pe.wait_ge(l1_evacuated, i * HALVES + 2)
                layer1(i, L1_ODD)
            i = TILES - 1
            pe.wait_ge(l0_evacuated, i * HALVES + 1)
            layer0(i, L0_ODD)
            pe.wait_ge(l1_evacuated, i * HALVES + 1)
            layer1(i, L1_EVEN)
            pe.wait_ge(l1_evacuated, i * HALVES + 2)
            layer1(i, L1_LAST)

            def head1(q):
                cols = slice(q * BANK, (q + 1) * BANK)
                pe.wait_ge(reduced0, TILES_PER_Q * HALVES * (q + 1) + 1)
                pe.wait_ge(reduced1, TILES_PER_Q * HALVES * (q + 1) + 1)
                for m in range(M1):
                    if q > 0:
                        pe.wait_ge(h1_ready, M1 * (q - 1) + m + 1)
                    for kt, feat in enumerate((feat_a, feat_b)):
                        last = nc.tensor.matmul(head_banks[m], wt1_sb[:, kt, m * P:(m + 1) * P], feat[:, cols],
                                                start=(kt == 0), stop=(kt == 1))
                    last.then_inc(h1_summed, 1)

            def head2(q):
                pe.wait_ge(h1_ready, M1 * (q + 1))
                for m in range(M2):
                    if q > 0:
                        pe.wait_ge(h2_ready, M2 * (q - 1) + m + 1)
                    for kt in range(M1):
                        last = nc.tensor.matmul(head_banks[M1 + m], wt2_sb[:, kt, m * P:(m + 1) * P],
                                                h1_sb[:, q % 2, kt, :], start=(kt == 0), stop=(kt == M1 - 1))
                    last.then_inc(h2_summed, 1)

            def head3(q):
                pe.wait_ge(h2_ready, M2 * (q + 1))
                if q == 0:
                    pe.wait_ge(l1_evacuated, TILES * HALVES + 1)
                else:
                    pe.wait_ge(y_ready, q)
                for kt in range(M2):
                    last = nc.tensor.matmul(head_banks[M1 + M2][0:1, :], wt3_sb[:, kt:kt + 1],
                                            h2_sb[:, q % 2, kt, :], start=(kt == 0), stop=(kt == M2 - 1))
                last.then_inc(y_summed, 1)

            pe.wait_ge(dense_in, 16)
            pe.wait_ge(head_weights_in, 32)
            pe.wait_ge(x_staged, TILES * HALVES)
            pe.wait_ge(l0_evacuated, TILES * HALVES)
            for q in range(QB + 2):
                if q < QB:
                    head1(q)
                if 1 <= q <= QB:
                    head2(q - 1)
                if q >= 2:
                    head3(q - 2)

        @block.scalar
        def _(act):
            def stage_x(i):
                for h in range(HALVES):
                    act.wait_ge(x_transposed, i * HALVES + h + 1)
                    nc.scalar.activation(x_stage[h * 64:h * 64 + F, :], ps_x[0:F, h, :], ACT.Copy)\
                        .then_inc(x_staged, 1)

            def highs(steps, rows, i, turn, which):
                done = before(i, turn)
                for order, (formed, unit) in list(enumerate(split_units(steps)))[which]:
                    act.wait_ge(units_formed, done.units + formed)
                    if not isinstance(done.splits, int) or done.splits + order >= NSPLIT:
                        act.wait_ge(splits_used, done.splits + (order + 1 - NSPLIT))
                    nc.scalar.activation(high_ring[0:rows, (turn.splits + order) % NSPLIT, 0:len(unit), :],
                                         split_whole[0:rows, 0:len(unit), :], ACT.Copy).then_inc(highs_formed, 1)

            def highs0(i, turn):
                highs(STEPS0, P0, i, turn, slice(None))

            def highs1(i, turn, which):
                highs(STEPS1, P, i, turn, which)

            def evacuate0(i, turn):
                act.wait_ge(splits_used, before(i, turn).splits + C0.splits)
                nc.scalar.activation(l0_cols, ps_0[:], ACT.Relu, bias=b0_sb[:]).then_inc(l0_evacuated, 1)

            def evacuate1(i, turn):
                act.wait_ge(splits_used, before(i, turn).splits + C1.splits)
                nc.scalar.activation(l1_cols, ps_1[:], ACT.Relu, bias=b1_sb[:]).then_inc(l1_evacuated, 1)

            act.sem_inc(l1_evacuated, 1)
            act.wait_ge(consts_in, CONSTS_LANDED)
            nc.scalar.activation(w1_high[:], w1_split_in, ACT.Copy).then_inc(weights_high, 1)
            act.wait_ge(weights_summed, 2)
            nc.scalar.activation(w0_high[:], w0_split_in[:, 0, :, :], ACT.Copy).then_inc(weights_high, 1)
            stage_x(0)
            highs0(0, PROLOGUE)
            act.wait_ge(reduced0, 1)
            evacuate0(0, PROLOGUE)
            with act.Fori(0, TILES - 1) as i:
                highs0(i, L0_ODD)
                highs1(i, L1_EVEN, slice(0, AHEAD))
                act.wait_ge(y_written[0], (i + 1) * 16)
                act.wait_ge(reduced0, i * HALVES + 2)
                evacuate0(i, L0_ODD)
                for h in range(HALVES):
                    act.wait_ge(x_written[h], (i + 1) * (16 * len(COPIES)))
                stage_x(i + 1)
                highs1(i, L1_EVEN, slice(AHEAD, None))
                act.wait_ge(reduced1, i * HALVES + 1)
                evacuate1(i, L1_EVEN)
                highs0(i, L0_EVEN)
                highs1(i, L1_ODD, slice(0, AHEAD))
                act.wait_ge(y_written[1], (i + 1) * 16)
                act.wait_ge(reduced0, i * HALVES + 3)
                evacuate0(i, L0_EVEN)
                highs1(i, L1_ODD, slice(AHEAD, None))
                act.wait_ge(reduced1, i * HALVES + 2)
                evacuate1(i, L1_ODD)
            i = TILES - 1
            highs0(i, L0_ODD)
            highs1(i, L1_EVEN, slice(0, AHEAD))
            act.wait_ge(y_written[0], (i + 1) * 16)
            act.wait_ge(reduced0, i * HALVES + 2)
            evacuate0(i, L0_ODD)
            highs1(i, L1_EVEN, slice(AHEAD, None))
            act.wait_ge(reduced1, i * HALVES + 1)
            evacuate1(i, L1_EVEN)
            highs1(i, L1_LAST, slice(None))
            act.wait_ge(reduced1, i * HALVES + 2)
            evacuate1(i, L1_LAST)

            def take1(q):
                if q >= 2:
                    act.wait_ge(h2_summed, M2 * (q - 1))
                for m in range(M1):
                    act.wait_ge(h1_summed, M1 * q + m + 1)
                    nc.scalar.activation(h1_sb[:, q % 2, m, :], head_banks[m], ACT.Relu,
                                         bias=bt1_sb[:, m:m + 1]).then_inc(h1_ready, 1)

            def take2(q):
                if q >= 2:
                    act.wait_ge(y_summed, q - 1)
                for m in range(M2):
                    act.wait_ge(h2_summed, M2 * q + m + 1)
                    nc.scalar.activation(h2_sb[:, q % 2, m, :], head_banks[M1 + m], ACT.Relu,
                                         bias=bt2_sb[:, m:m + 1]).then_inc(h2_ready, 1)

            for q in range(QB + 1):
                if q < QB:
                    take1(q)
                if q >= 1:
                    take2(q - 1)

        @block.vector
        def _(dve):
            def form(out, unit, left, right, done):
                def operand(tiles, indices):
                    if len(set(indices)) == 1:
                        one = tiles[:, indices[0], :].unsqueeze(1)
                        return one if len(indices) == 1 else one.broadcast_to([one.shape[0], 2, COLS])
                    return tiles[:, indices[0]:indices[1] + 1:indices[1] - indices[0], :]
                nc.vector.tensor_tensor(out[:, 0:len(unit), :], operand(left, [a for a, _ in unit]),
                                        operand(right, [b for _, b in unit]), ALU.mult).then_inc(units_formed, 1)

            def layer(steps, rows, left, right, done, turn, arrived, between=()):
                plains = splits = 0
                for step, (split_unit, plain_unit) in enumerate(steps):
                    if split_unit is not None:
                        arrived(split_unit)
                        if not isinstance(done.splits, int) or done.splits + splits >= 1:
                            dve.wait_ge(lows_formed, done.splits + splits)
                        form(split_whole[0:rows], split_unit, left, right, done)
                    arrived(plain_unit)
                    if not isinstance(done.plains, int) or done.plains + plains >= NPLAIN:
                        dve.wait_ge(plains_used, done.plains + (plains + 1 - NPLAIN))
                    form(plain_ring[0:rows, (turn.plains + plains) % NPLAIN], plain_unit, left, right, done)
                    plains += 1
                    if split_unit is not None:
                        n = len(split_unit)
                        slot = (turn.splits + splits) % NSPLIT
                        splits += 1
                        dve.wait_ge(highs_formed, done.splits + splits)
                        nc.vector.tensor_tensor(low_ring[0:rows, slot, 0:n, :], split_whole[0:rows, 0:n, :],
                                                high_ring[0:rows, slot, 0:n, :].bitcast(F32),
                                                ALU.subtract).then_inc(lows_formed, 1)
                    if step >= REDUCE_AT and step - REDUCE_AT < len(between):
                        between[step - REDUCE_AT]()

            def layer0(i, turn, tile, h):
                waited = set()

                def arrived(unit):
                    for j in sorted({j for pair in unit for j in pair} - waited):
                        dve.wait_ge(x_loaded[j], (tile * HALVES + h + 1) * 16)
                        waited.add(j)

                layer(STEPS0, P0, x_tiles, x_tiles, before(i, turn), turn, arrived)

            def layer1(i, turn, h, between=()):
                waited = set()

                def arrived(unit):
                    for k, j in unit:
                        if ("s", k) not in waited:
                            dve.wait_ge(s_loaded[h][k], (i + 1) * 16)
                        if ("t", j) not in waited:
                            dve.wait_ge(t_loaded[h][j], (i + 1) * 16)
                        waited.update((("s", k), ("t", j)))

                layer(STEPS1, P, s_tiles[:, h], t_tiles[:, h], before(i, turn), turn, arrived, between)

            def reduce_dims(rows, result, i, h, start, done):
                if h == 0:
                    dve.wait_ge(done, i * HALVES + start)
                    rows, result = rows[:, 0:DH, :], rows[:, DH, :]
                else:
                    dve.wait_ge(done, i * HALVES + 1 + start)
                nc.vector.tensor_reduce(result, rows.rearrange("p d b -> p b d"), AX_X, ALU.add).then_inc(done, 1)

            def reduce0(i, h):
                dve.wait_ge(l0_evacuated, i * HALVES + h + 1)
                reduce_dims(l0_out[H1:P], feat_b[H1:P, bass.ds(i * P, P)], i, h, 1, reduced0)

            def reduce1(i, h):
                dve.wait_ge(l1_evacuated, i * HALVES + h + 2)
                reduce_dims(l1_out[:], feat_a[:, bass.ds(i * P, P)], i, h, 1, reduced1)

            nc.vector.memset(feat_b[0:H1, :], 0.0).then_inc(feat_zeroed, 1)
            dve.wait_ge(consts_in, CONSTS_LANDED)
            nc.vector.tensor_tensor(w0_sb[:], w0_plain_in[:, 0], w0_plain_in[:, 1], ALU.add).then_inc(weights_summed, 1)
            nc.vector.tensor_tensor(w0_split_in[:, 0], w0_split_in[:, 0], w0_split_in[:, 1],
                                    ALU.add).then_inc(weights_summed, 1)
            dve.wait_ge(weights_high, 1)
            nc.vector.tensor_tensor(w1_low[:], w1_split_in, w1_high[:].bitcast(F32), ALU.subtract)\
                .then_inc(weights_split, 1)
            dve.wait_ge(weights_high, 2)
            nc.vector.tensor_tensor(w0_low[:], w0_split_in[:, 0], w0_high[:].bitcast(F32), ALU.subtract)\
                .then_inc(weights_split, 1)
            dve.wait_ge(weights_split, 2)
            dve.sem_inc(reduced1, 1)
            dve.sem_inc(reduced0, 1)
            layer0(0, PROLOGUE, 0, 0)
            layer0(0, L0_ODD, 0, 1)
            reduce0(0, 0)
            layer1(0, L1_EVEN, 0, (lambda: reduce0(0, 1),))
            layer0(0, L0_EVEN, 1, 0)
            layer1(0, L1_ODD, 1, (lambda: reduce1(0, 0), lambda: reduce0(1, 0)))
            with dve.Fori(1, TILES - 1) as i:
                layer0(i, L0_ODD, i, 1)
                layer1(i, L1_EVEN, 0, (lambda: reduce1(i - 1, 1), lambda: reduce0(i, 1)))
                layer0(i, L0_EVEN, i + 1, 0)
                layer1(i, L1_ODD, 1, (lambda: reduce1(i, 0), lambda: reduce0(i + 1, 0)))
            i = TILES - 1
            layer0(i, L0_ODD, i, 1)
            layer1(i, L1_EVEN, 0, (lambda: reduce1(i - 1, 1), lambda: reduce0(i, 1)))
            layer1(i, L1_LAST, 1, (lambda: reduce1(i, 0),))
            reduce1(i, 1)
            for q in range(QB):
                dve.wait_ge(y_summed, q + 1)
                nc.vector.tensor_copy(y_sb[:, q * BANK:(q + 1) * BANK],
                                      head_banks[M1 + M2][0:1, :]).then_inc(y_ready, 1)


def shifts(j, r):
    base, step = SHIFT_BASE_STEP[j]
    return [(r + base + step * g) % F for g in range(GROUPS)]


def layer0_rows():
    pairs = PLAIN0 + SPLIT0
    forward = np.full((P0, len(pairs)), -1)
    backward = np.full((P0, len(pairs)), -1)
    seen = set()
    for n, (a, b) in enumerate(pairs):
        for r in range(F):
            for g, (h, m) in enumerate(zip(shifts(a, r), shifts(b, r))):
                if (min(h, m), max(h, m)) in seen:
                    continue
                seen.add((min(h, m), max(h, m)))
                forward[r * GROUPS + g, n] = h * F + m
                if h != m:
                    backward[r * GROUPS + g, n] = m * F + h
    assert len(seen) == F * (F + 1) // 2
    return forward, backward


def layer1_rows():
    pairs = PLAIN1 + SPLIT1
    place = np.full((P, len(pairs)), -1)
    for p in range(P):
        u, v = divmod(p, VX)
        for n, (k, j) in enumerate(pairs):
            if RX * v + k < F:
                place[p, n] = (RY * u + j) * F + RX * v + k
    return place


def rows_or_zero(w, place):
    laid = np.zeros(place.shape + (w.shape[0],), w.dtype)
    laid[place >= 0] = w.T[place[place >= 0]]
    return laid


def kernel(**inputs):
    import concourse.bacc as bacc
    from concourse.bass_utils import run_bass_kernel_spmd

    a = {name: np.asarray(x) for name, x in inputs.items()}
    forward, backward = layer0_rows()
    w0 = np.stack([rows_or_zero(a["L0_rec_W0"], place) for place in (forward, backward)], axis=1)
    w1 = rows_or_zero(a["L0_rec_W1"], layer1_rows())
    w_top1 = np.zeros((P, 2, HID1), a["W_top1"].dtype)
    w_top1[:, 0] = a["W_top1"][H1:H1 + OUT]
    w_top1[0:D, 1] = a["W_top1"][H1 + OUT:]
    w_top1[H1:, 1] = a["W_top1"][0:H1]
    arrays = {
        "dense_t": a["dense_ctx"].T,
        "ids": a["ids"].reshape(TILES, P, F),
        "w0_plain": w0[:, :, :len(PLAIN0)],
        "w0_split": w0[:, :, len(PLAIN0):],
        "b0": a["L0_rec_b0"].reshape(P, 1),
        "w1_plain": w1[:, :len(PLAIN1)],
        "w1_split": w1[:, len(PLAIN1):],
        "b1": a["L0_rec_b1"].reshape(P, 1),
        "wt1": w_top1,
        "bt1": a["b_top1"].reshape(M1, P).T,
        "wt2": a["W_top2"].reshape(M1, P, HID2).transpose(1, 0, 2),
        "bt2": a["b_top2"].reshape(M2, P).T,
        "wt3": a["W_top3"].reshape(M2, P).T,
        "ident": np.eye(P, dtype=np.float32),
    }
    arrays |= {f"tbl_{f}": a[f"tbl_{f}"] for f in range(F)}
    arrays = {f"in_{name}": np.ascontiguousarray(x) for name, x in arrays.items()}
    nc = bacc.Bacc("TRN2", target_bir_lowering=False, num_devices=1)
    aps = {name: nc.dram_tensor(name, x.shape, mybir.dt.from_np(x.dtype), kind="ExternalInput").ap()
           for name, x in arrays.items()}
    out = nc.dram_tensor("out_y", (B, 1), F32, kind="ExternalOutput").ap()
    names = ("dense_t", "ids", "w0_plain", "w0_split", "b0", "w1_plain", "w1_split", "b1", "wt1", "bt1", "wt2", "bt2", "wt3", "ident")
    interaction_kernel(nc, tables=[aps[f"in_tbl_{f}"] for f in range(F)], out=out,
                       **{name: aps[f"in_{name}"] for name in names})
    result = run_bass_kernel_spmd(nc, [arrays], core_ids=[0])
    return result.results[0]["out_y"]
```

```python
from collections import namedtuple
from contextlib import ExitStack

import concourse.bass as bass
import numpy as np
from concourse import mybir

F32 = mybir.dt.float32
F32R = mybir.dt.float32r
I32 = mybir.dt.int32
ALU = mybir.AluOpType
ACT = mybir.ActivationFunctionType
AX_X = mybir.AxisListType.X

P = 128
B, F, D = 2048, 39, 16
H1, OUT = 64, 128
TILES = B // P
HALVES = 2
DH = D // HALVES
COLS = P * DH
BANK = 512
NBANK = COLS // BANK

GROUPS = 3
P0 = GROUPS * F
SHIFT_BASE_STEP = [(0, 0), (35, 5), (4, 22), (0, 5), (28, 0)]
NX = len(SHIFT_BASE_STEP)
XROWS = max(b + s * (GROUPS - 1) for b, s in SHIFT_BASE_STEP) + F

XD = F * D
PIECES = -(-XD // P)
LAST_PIECE = XD - (PIECES - 1) * P
TAIL_PIECES = -(-(XROWS - 2 * F) * D // P)
assert 0 < TAIL_PIECES < PIECES
X_WRITES = 2 * 2 + 1

RY, RX, UY, VX = 4, 5, 16, 8

UNITS0 = [[(0, 2), (1, 2)], [(1, 4), (2, 4)], [(3, 4)], [(0, 1), (0, 3)]]
UNITS1 = [[(k, j), (k, j + 1)] for k in range(RX) for j in range(0, RY, 2)]
SPLIT_AT0, SPLIT_AT1 = (2,), (1, 3, 6, 8)


def steps_of(units, split_at):
    return [(units[n - 1] if n - 1 in split_at else None, unit)
            for n, unit in enumerate(units) if n not in split_at]


STEPS0, STEPS1 = steps_of(UNITS0, SPLIT_AT0), steps_of(UNITS1, SPLIT_AT1)
REDUCE_AT = 1
AHEAD = 1
NUNIT, NSPLIT = 4, 2

HID1, HID2 = 512, 256
M1, M2 = HID1 // P, HID2 // P
QB = B // BANK
TILES_PER_Q = TILES // QB

Count = namedtuple("Count", "units plains splits")


def size(steps):
    splits = sum(split is not None for split, _ in steps)
    return Count(len(steps) + splits, len(steps), splits)


def kinds(steps):
    return [split for first, _ in steps for split in ((False,) if first is None else (True, False))]


def plus(*counts):
    return Count(*(sum(column) for column in zip(*counts)))


def split_units(steps):
    found, formed = [], 0
    for split, _ in steps:
        if split is not None:
            found.append((formed + 1, split))
        formed += 1 if split is None else 2
    return found


C0, C1 = size(STEPS0), size(STEPS1)
PROLOGUE = Count(0, 0, 0)
L0_ODD = C0
L1_EVEN = plus(C0, C0)
L0_EVEN = L1_LAST = plus(C0, C0, C1)
L1_ODD = plus(C0, C0, C1, C0)
PER_TILE = plus(C0, C0, C1, C1)
assert PER_TILE.units % NUNIT == 0 and PER_TILE.splits % NSPLIT == 0


ALL = plus(*[PER_TILE] * TILES)


def before(i, turn):
    return Count(*(i * per + at for per, at in zip(PER_TILE, turn)))


def products_of(steps, split):
    return sorted(pair for step in steps for pair in (step[0] if split else step[1]) or ())


PLAIN0, SPLIT0 = products_of(STEPS0, False), products_of(STEPS0, True)
PLAIN1, SPLIT1 = products_of(STEPS1, False), products_of(STEPS1, True)


def interaction_kernel(nc, *, dense_t, ids, tables, w0_plain, w0_split, b0, w1_plain, w1_split, b1,
                       wt1, bt1, wt2, bt2, wt3, ident, out):
    with ExitStack() as ctx:
        def sb(name, shape, dt=F32):
            return ctx.enter_context(nc.sbuf_tensor(name, shape, dt))

        def ps(name, shape):
            return ctx.enter_context(nc.psum_tensor(name, shape, F32))

        def sem(name):
            return ctx.enter_context(nc.semaphore(name))

        x_dram = nc.dram_tensor("x_rows", [TILES, 2 * XD + TAIL_PIECES * P, P], F32, kind="Internal").ap()
        y_dram = nc.dram_tensor("y_rows", [TILES, HALVES, H1, COLS], F32, kind="Internal").ap()

        ident_sb = sb("ident_sb", [P, P])
        ids_now = sb("ids_now", [P, F], I32)
        ids_1 = sb("ids_1", [P, F], I32)
        emb = sb("emb", [P, XD])
        x_stage = sb("x_stage", [P, PIECES, P])
        x_tiles = sb("x_tiles", [P0, NX, COLS])
        s_tiles = sb("s_tiles", [P, HALVES, RX, COLS])
        t_tiles = sb("t_tiles", [P, HALVES, RY, COLS])
        unit_ring = sb("unit_ring", [P, NUNIT, 2, COLS])
        high_ring = sb("high_ring", [P, NSPLIT, 2, COLS], F32R)
        low_ring = sb("low_ring", [P, NSPLIT, 2, COLS], F32R)
        l0_out = sb("l0_out", [P, DH + 1, P])
        l1_out = sb("l1_out", [P, DH + 1, P])
        l0_cols = l0_out[:, 0:DH, :].rearrange("p d b -> p (d b)")
        l1_cols = l1_out[:, 0:DH, :].rearrange("p d b -> p (d b)")
        w0_sb = sb("w0_sb", [P0, len(PLAIN0), OUT])
        w0_high = sb("w0_high", [P0, len(SPLIT0), OUT], F32R)
        w0_low = sb("w0_low", [P0, len(SPLIT0), OUT], F32R)
        w1_sb = sb("w1_sb", [P, len(PLAIN1), OUT])
        w1_high = sb("w1_high", [P, len(SPLIT1), OUT], F32R)
        w1_low = sb("w1_low", [P, len(SPLIT1), OUT], F32R)
        b0_sb = sb("b0_sb", [P, 1])
        b1_sb = sb("b1_sb", [P, 1])
        feat_a = sb("feat_a", [P, B])
        feat_b = sb("feat_b", [P, B])
        wt3_sb = sb("wt3_sb", [P, M2])
        bt1_sb = sb("bt1_sb", [P, M1])
        bt2_sb = sb("bt2_sb", [P, M2])

        w0_plain_in = unit_ring[0:P0, 0, :, :].rearrange("p a c -> p (a c)")[:, 0:2 * len(PLAIN0) * OUT]
        w0_plain_in = w0_plain_in.rearrange("p (o n c) -> p o n c", o=2, c=OUT)
        w0_split_in = unit_ring[0:P0, 1, :, :].rearrange("p a c -> p (a c)")[:, 0:2 * len(SPLIT0) * OUT]
        w0_split_in = w0_split_in.rearrange("p (o n c) -> p o n c", o=2, c=OUT)
        w1_split_in = l1_cols[:, 0:len(SPLIT1) * OUT]
        w1_split_in = w1_split_in.rearrange("p (n c) -> p n c", c=OUT)

        emb_1 = l1_cols[:, 0:XD]

        wt1_sb = s_tiles[:, 0, 0, :].rearrange("p (a c) -> p a c", c=HID1)
        wt2_sb = s_tiles[:, 0, 1, :].rearrange("p (a c) -> p a c", c=HID2)
        h1_sb = unit_ring[:, 0].rearrange("p n (q c) -> p (n q) c", c=BANK)
        h2_sb = unit_ring[:, 1].rearrange("p b (m c) -> p b m c", c=BANK)
        EARLY, LATE = (ALL.splits - 2) % NSPLIT, (ALL.splits - 1) % NSPLIT
        wt1_high, wt1_low = (ring[:, EARLY, 0, :].rearrange("p (a c) -> p a c", c=HID1)
                             for ring in (high_ring, low_ring))
        feat_high, feat_low = (ring[:, EARLY, 1, :].rearrange("p (a c) -> p a c", c=BANK)
                               for ring in (high_ring, low_ring))
        h1_high, h1_low = (ring[:, LATE].rearrange("p n (q c) -> p (n q) c", c=BANK)
                           for ring in (high_ring, low_ring))
        wt2_high, wt2_low = (part[:].rearrange("p n c -> p (n c)")[:, 0:M1 * HID2]
                             .rearrange("p (a c) -> p a c", c=HID2) for part in (w1_high, w1_low))
        y_sb = feat_b[0:1, :]

        ps_x = ps("ps_x", [P, HALVES * COLS])
        ps_0 = ps("ps_0", [P, COLS])
        ps_1 = ps("ps_1", [P, COLS])
        head_banks = [acc[:, q * BANK:(q + 1) * BANK]
                      for acc in (ps_x[:, 0:COLS], ps_x[:, COLS:], ps_0, ps_1) for q in range(2)]

        consts_in = sem("consts_in")
        ids_in = sem("ids_in")
        first_ids_in = [sem("ids_0_in"), sem("ids_1_in")]
        gathered = sem("gathered")
        gathered_1 = sem("gathered_1")
        gather_begun = sem("gather_begun")
        transpose_begun = sem("transpose_begun")
        weights_summed = sem("weights_summed")
        weights_high = sem("weights_high")
        weights_split = sem("weights_split")
        feat_zeroed = sem("feat_zeroed")
        dense_in = sem("dense_in")
        x_transposed = sem("x_transposed")
        x_staged = sem("x_staged")
        x_written = sem("x_written")
        x_loaded = [sem(f"x_loaded{j}") for j in range(NX)]
        s_loaded = [[sem(f"s_loaded{h}_{k}") for k in range(RX)] for h in range(HALVES)]
        t_loaded = [[sem(f"t_loaded{h}_{j}") for j in range(RY)] for h in range(HALVES)]
        y_written = [sem(f"y_written{h}") for h in range(HALVES)]
        units_formed = sem("units_formed")
        highs_formed = sem("highs_formed")
        lows_formed = sem("lows_formed")
        plains_used = sem("plains_used")
        splits_used = sem("splits_used")
        l0_evacuated = sem("l0_evacuated")
        l1_evacuated = sem("l1_evacuated")
        reduced0 = sem("reduced0")
        reduced1 = sem("reduced1")
        head_weights_in = sem("head_weights_in")
        wt1_high_ready = sem("wt1_high_ready")
        wt1_split = sem("wt1_split")
        wt2_high_ready = sem("wt2_high_ready")
        wt2_split = sem("wt2_split")
        feat_highs_formed = sem("feat_highs_formed")
        feat_lows_formed = sem("feat_lows_formed")
        h1_summed = sem("h1_summed")
        h1_ready = sem("h1_ready")
        h1_highs_formed = sem("h1_highs_formed")
        h1_lows_formed = sem("h1_lows_formed")
        h1_used = sem("h1_used")
        h2_ready = sem("h2_ready")
        y_summed = sem("y_summed")
        y_ready = sem("y_ready")
        y_out = sem("y_out")

        consts = ((ident_sb, ident), (w0_plain_in, w0_plain), (w0_split_in, w0_split), (b0_sb, b0),
                  (w1_split_in, w1_split), (w1_sb, w1_plain), (b1_sb, b1), (wt3_sb, wt3), (bt1_sb, bt1),
                  (bt2_sb, bt2))
        CONSTS_LANDED = 16 * len(consts)

        block = ctx.enter_context(nc.Block())

        def x_view(i, h, j):
            base, step = SHIFT_BASE_STEP[j]
            rows = x_dram[i]
            return bass.AP(rows.tensor, rows.offset + base * (D * P) + h * COLS,
                           [[D * P, F], [step * D * P, GROUPS], [1, COLS]])

        def s_view(i, h, k):
            rows = x_dram[i]
            return bass.AP(rows.tensor, rows.offset + k * (D * P) + h * COLS,
                           [[0, UY], [RX * D * P, VX], [1, COLS]])

        def t_view(i, h, j):
            rows = y_dram[i, h]
            return bass.AP(rows.tensor, rows.offset + j * COLS, [[RY * COLS, UY], [0, VX], [1, COLS]])

        @block.sync
        def _(sp):
            for i, to in enumerate((ids_now, ids_1)):
                sp.dma_start(to[:], ids[i]).then_inc(first_ids_in[i], 16)
            for dst, src in consts:
                sp.dma_start(dst[:], src).then_inc(consts_in, 16)
            sp.wait_ge(feat_zeroed, 1)
            sp.dma_start(feat_b[0:D, :], dense_t).then_inc(dense_in, 16)

            def write_x(i):
                sp.wait_ge(x_staged, i + 1)

                def write(line, first, count, lines=P):
                    to = x_dram[i, line:line + (count - 1) * P + lines].rearrange("(t p) b -> p t b", p=lines)
                    sp.dma_start(to, x_stage[0:lines, first:first + count, :]).then_inc(x_written, 16)

                for copy in range(2):
                    write(copy * XD, 0, PIECES - 1)
                    write(copy * XD + (PIECES - 1) * P, PIECES - 1, 1, LAST_PIECE)
                write(2 * XD, 0, TAIL_PIECES)

            def load_x(i, h, last_use=None):
                written = i * (16 * X_WRITES) + 16 * X_WRITES
                if last_use is not None:
                    sp.wait_ge(units_formed, last_use)
                sp.wait_ge(x_written, written)
                for j in (2, 0, 1, 4, 3):
                    sp.dma_start(x_tiles[:, j, :], x_view(i, h, j)).then_inc(x_loaded[j], 16)

            def load_s(i, h, turn=None):
                for k in range(RX):
                    if turn is not None:
                        sp.wait_ge(units_formed, turn.units + 2 * (k + 1))
                    sp.dma_start(s_tiles[:, h, k, :], s_view(i, h, k)).then_inc(s_loaded[h][k], 16)

            def write_y(i, h):
                sp.wait_ge(l0_evacuated, i * HALVES + h + 1)
                sp.dma_start(y_dram[i, h], l0_cols[0:H1, :]).then_inc(y_written[h], 16)

            def load_t(i, h):
                sp.wait_ge(y_written[h], 16 * (i + 1))
                for j in range(RY):
                    sp.dma_start(t_tiles[:, h, j, :], t_view(i, h, j)).then_inc(t_loaded[h][j], 16)

            write_x(0)
            load_x(0, 0)
            load_s(0, 0)
            load_x(0, 1, C0.units)
            write_y(0, 0)
            load_t(0, 0)
            load_s(0, 1)
            write_y(0, 1)
            load_t(0, 1)
            with sp.Fori(0, TILES - 1) as i:
                write_x(i + 1)
                load_x(i + 1, 0, before(i, L1_EVEN).units)
                load_s(i + 1, 0, before(i, L1_EVEN))
                write_y(i + 1, 0)
                load_t(i + 1, 0)
                load_x(i + 1, 1, before(i, L1_ODD).units)
                load_s(i + 1, 1, before(i, L1_ODD))
                write_y(i + 1, 1)
                load_t(i + 1, 1)
            sp.wait_ge(units_formed, before(TILES - 1, L1_LAST).units)
            sp.dma_start(wt1_sb, wt1).then_inc(head_weights_in, 16)
            sp.dma_start(wt2_sb, wt2).then_inc(head_weights_in, 16)
            sp.wait_ge(y_ready, QB)
            sp.dma_start(out.rearrange("b o -> o b"), y_sb).then_inc(y_out, 16)
            sp.wait_ge(y_out, 16)

        @block.gpsimd
        def _(pool):
            def gather(ids_of_tile, to, done):
                pool.sem_inc(gather_begun, 1)
                for f in range(F):
                    nc.gpsimd.indirect_dma_start(
                        out=to[:, f * D:(f + 1) * D], out_offset=None, in_=tables[f],
                        in_offset=bass.IndirectOffsetOnAxis(ap=ids_of_tile[:, f:f + 1], axis=0),
                    ).then_inc(done, 16)

            pool.wait_ge(first_ids_in[0], 16)
            gather(ids_now, emb, gathered)
            pool.wait_ge(first_ids_in[1], 16)
            pool.wait_ge(weights_split, 2)
            gather(ids_1, emb_1, gathered_1)
            with pool.Fori(2, TILES) as i:
                pool.wait_ge(x_transposed, i)
                pool.dma_start(ids_now[:], ids[i]).then_inc(ids_in, 16)
                pool.wait_ge(ids_in, (i - 1) * 16)
                gather(ids_now, emb, gathered)

        @block.tensor
        def _(pe):
            def transpose_x(rows):
                pe.sem_inc(transpose_begun, 1)
                for t in range(PIECES):
                    lines = P if t < PIECES - 1 else LAST_PIECE
                    last = nc.tensor.transpose(ps_x[0:lines, t * P:(t + 1) * P], rows[:, t * P:t * P + lines],
                                               ident_sb[:])
                last.then_inc(x_transposed, 1)

            def plain(acc, unit, weights, order, slot, rows, first, last):
                for n, pair in enumerate(unit):
                    for q in range(NBANK):
                        cols = slice(q * BANK, (q + 1) * BANK)
                        mm = nc.tensor.matmul(acc[:, cols], weights[:, order.index(pair), :],
                                              unit_ring[0:rows, slot, n, cols],
                                              start=(first and n == 0), stop=(last and n == len(unit) - 1))
                mm.then_inc(plains_used, 1)

            def split(acc, unit, high, low, order, slot, rows, last):
                for n, pair in enumerate(unit):
                    passes = ((high, high_ring), (low, high_ring), (high, low_ring))
                    for m, (weights, ring) in enumerate(passes):
                        for q in range(NBANK):
                            cols = slice(q * BANK, (q + 1) * BANK)
                            mm = nc.tensor.matmul(acc[:, cols], weights[:, order.index(pair), :],
                                                  ring[0:rows, slot, n, cols], start=False,
                                                  stop=(last and n == len(unit) - 1 and m == 2))
                mm.then_inc(splits_used, 1)

            def layer(acc, steps, rows, weights, orders, done, turn):
                whole, high, low = weights
                splits = units = 0
                for step, (split_unit, plain_unit) in enumerate(steps):
                    end = step == len(steps) - 1
                    units += 1 if split_unit is None else 2
                    pe.wait_ge(units_formed, done.units + units)
                    plain(acc, plain_unit, whole, orders[0], (turn.units + units - 1) % NUNIT, rows,
                          step == 0, end and split_unit is None)
                    if split_unit is not None:
                        pe.wait_ge(lows_formed, done.splits + (splits + 1))
                        split(acc, split_unit, high, low, orders[1], (turn.splits + splits) % NSPLIT, rows, end)
                        splits += 1

            def layer0(i, turn):
                layer(ps_0, STEPS0, P0, (w0_sb, w0_high, w0_low), (PLAIN0, SPLIT0), before(i, turn), turn)

            def layer1(i, turn):
                layer(ps_1, STEPS1, P, (w1_sb, w1_high, w1_low), (PLAIN1, SPLIT1), before(i, turn), turn)

            pe.wait_ge(consts_in, CONSTS_LANDED)
            pe.wait_ge(gathered, 16 * F)
            transpose_x(emb)
            pe.wait_ge(weights_split, 2)
            layer0(0, PROLOGUE)

            def tile(i, next_rows, next_gathered, count):
                pe.wait_ge(l0_evacuated, i * HALVES + 1)
                layer0(i, L0_ODD)
                pe.wait_ge(x_staged, i + 1)
                pe.wait_ge(next_gathered, count)
                transpose_x(next_rows)
                pe.wait_ge(l1_evacuated, i * HALVES + 1)
                layer1(i, L1_EVEN)
                pe.wait_ge(l0_evacuated, i * HALVES + 2)
                layer0(i, L0_EVEN)
                pe.wait_ge(l1_evacuated, i * HALVES + 2)
                layer1(i, L1_ODD)

            tile(0, emb_1, gathered_1, 16 * F)
            with pe.Fori(1, TILES - 1) as i:
                tile(i, emb, gathered, (i + 1) * (16 * F))
            i = TILES - 1
            pe.wait_ge(l0_evacuated, i * HALVES + 1)
            layer0(i, L0_ODD)
            pe.wait_ge(l1_evacuated, i * HALVES + 1)
            layer1(i, L1_EVEN)
            pe.wait_ge(l1_evacuated, i * HALVES + 2)
            layer1(i, L1_LAST)

            def three_passes(out, high, low, moving_high, moving_low, first, last):
                nc.tensor.matmul(out, high, moving_high, start=first, stop=False)
                nc.tensor.matmul(out, low, moving_high, start=False, stop=False)
                return nc.tensor.matmul(out, high, moving_low, start=False, stop=last)

            def head1(q):
                pe.wait_ge(feat_lows_formed, 2 * (q + 1))
                for m in range(M1):
                    if q > 0:
                        pe.wait_ge(h1_ready, M1 * (q - 1) + m + 1)
                    part = slice(m * P, (m + 1) * P)
                    for kt in range(2):
                        mm = three_passes(head_banks[m], wt1_high[:, kt, part], wt1_low[:, kt, part],
                                          feat_high[:, kt, :], feat_low[:, kt, :], kt == 0, kt == 1)
                    mm.then_inc(h1_summed, 1)

            def head2(q):
                if q > 0:
                    pe.wait_ge(h2_ready, M2 * q)
                for kt in range(M1):
                    pe.wait_ge(h1_lows_formed, M1 * q + kt + 1)
                    for m in range(M2):
                        part = slice(m * P, (m + 1) * P)
                        mm = three_passes(head_banks[M1 + m], wt2_high[:, kt, part], wt2_low[:, kt, part],
                                          h1_high[:, kt, :], h1_low[:, kt, :], kt == 0, kt == M1 - 1)
                    mm.then_inc(h1_used, 1)

            def head3(q):
                pe.wait_ge(h2_ready, M2 * (q + 1))
                if q > 0:
                    pe.wait_ge(y_ready, q)
                for kt in range(M2):
                    mm = nc.tensor.matmul(head_banks[M1 + M2][0:1, :], wt3_sb[:, kt:kt + 1],
                                          h2_sb[:, q % 2, kt, :], start=(kt == 0), stop=(kt == M2 - 1))
                mm.then_inc(y_summed, 1)

            pe.wait_ge(wt1_split, 1)
            pe.wait_ge(x_staged, TILES)
            head1(0)
            pe.wait_ge(l0_evacuated, TILES * HALVES)
            pe.wait_ge(l1_evacuated, TILES * HALVES + 1)
            pe.wait_ge(wt2_split, 1)
            head2(0)
            for q in range(1, QB):
                head1(q)
                head3(q - 1)
                head2(q)
            head3(QB - 1)

        @block.scalar
        def _(act):
            def stage_x(i):
                act.wait_ge(x_transposed, i + 1)
                whole = (PIECES - 1) * P
                nc.scalar.activation(x_stage[:, 0:PIECES - 1, :].rearrange("p t b -> p (t b)"), ps_x[:, 0:whole],
                                     ACT.Copy)
                nc.scalar.activation(x_stage[0:LAST_PIECE, PIECES - 1, :], ps_x[0:LAST_PIECE, whole:whole + P],
                                     ACT.Copy).then_inc(x_staged, 1)

            def highs(steps, rows, i, turn, which):
                done = before(i, turn)
                for order, (formed, unit) in list(enumerate(split_units(steps)))[which]:
                    act.wait_ge(units_formed, done.units + formed)
                    if not isinstance(done.splits, int) or done.splits + order >= NSPLIT:
                        act.wait_ge(splits_used, done.splits + (order + 1 - NSPLIT))
                    nc.scalar.activation(high_ring[0:rows, (turn.splits + order) % NSPLIT, 0:len(unit), :],
                                         unit_ring[0:rows, (turn.units + formed - 1) % NUNIT, 0:len(unit), :],
                                         ACT.Copy).then_inc(highs_formed, 1)

            def highs0(i, turn):
                highs(STEPS0, P0, i, turn, slice(None))

            def highs1(i, turn, which):
                highs(STEPS1, P, i, turn, which)

            def evacuate0(i, turn):
                act.wait_ge(splits_used, before(i, turn).splits + C0.splits)
                nc.scalar.activation(l0_cols, ps_0[:], ACT.Relu, bias=b0_sb[:]).then_inc(l0_evacuated, 1)

            def evacuate1(i, turn):
                act.wait_ge(splits_used, before(i, turn).splits + C1.splits)
                nc.scalar.activation(l1_cols, ps_1[:], ACT.Relu, bias=b1_sb[:]).then_inc(l1_evacuated, 1)

            act.sem_inc(l1_evacuated, 1)
            act.wait_ge(consts_in, CONSTS_LANDED)
            nc.scalar.activation(w1_high[:], w1_split_in, ACT.Copy).then_inc(weights_high, 1)
            act.wait_ge(weights_summed, 2)
            nc.scalar.activation(w0_high[:], w0_split_in[:, 0, :, :], ACT.Copy).then_inc(weights_high, 1)
            stage_x(0)
            highs0(0, PROLOGUE)
            act.wait_ge(reduced0, 1)
            evacuate0(0, PROLOGUE)

            def tile(i):
                highs0(i, L0_ODD)
                highs1(i, L1_EVEN, slice(0, AHEAD))
                act.wait_ge(y_written[0], (i + 1) * 16)
                act.wait_ge(reduced0, i * HALVES + 2)
                evacuate0(i, L0_ODD)
                act.wait_ge(x_written, (i + 1) * (16 * X_WRITES))
                stage_x(i + 1)
                highs1(i, L1_EVEN, slice(AHEAD, None))
                act.wait_ge(reduced1, i * HALVES + 1)
                evacuate1(i, L1_EVEN)
                highs0(i, L0_EVEN)
                highs1(i, L1_ODD, slice(0, AHEAD))
                act.wait_ge(y_written[1], (i + 1) * 16)
                act.wait_ge(reduced0, i * HALVES + 3)
                evacuate0(i, L0_EVEN)
                highs1(i, L1_ODD, slice(AHEAD, None))
                act.wait_ge(reduced1, i * HALVES + 2)
                evacuate1(i, L1_ODD)

            tile(0)
            with act.Fori(1, TILES - 1) as i:
                tile(i)
            i = TILES - 1
            highs0(i, L0_ODD)
            highs1(i, L1_EVEN, slice(0, AHEAD))
            act.wait_ge(y_written[0], (i + 1) * 16)
            act.wait_ge(reduced0, i * HALVES + 2)
            evacuate0(i, L0_ODD)
            highs1(i, L1_EVEN, slice(AHEAD, None))
            act.wait_ge(reduced1, i * HALVES + 1)
            evacuate1(i, L1_EVEN)
            highs1(i, L1_LAST, slice(None))

            def feat_highs(q):
                act.wait_ge(reduced0, TILES_PER_Q * HALVES * (q + 1) + 1)
                act.wait_ge(reduced1, TILES_PER_Q * HALVES * (q + 1) + 1)
                if q > 0:
                    act.wait_ge(h1_summed, M1 * q)
                for kt, feat in enumerate((feat_a, feat_b)):
                    nc.scalar.activation(feat_high[:, kt, :], feat[:, q * BANK:(q + 1) * BANK],
                                         ACT.Copy).then_inc(feat_highs_formed, 1)

            def take1(q):
                for m in range(M1):
                    act.wait_ge(h1_summed, M1 * q + m + 1)
                    if q > 0:
                        act.wait_ge(h1_lows_formed, M1 * (q - 1) + m + 1)
                    nc.scalar.activation(h1_sb[:, m, :], head_banks[m], ACT.Relu,
                                         bias=bt1_sb[:, m:m + 1]).then_inc(h1_ready, 1)
                    act.wait_ge(h1_ready, M1 * q + m + 1)
                    if q > 0:
                        act.wait_ge(h1_used, M1 * (q - 1) + m + 1)
                    nc.scalar.activation(h1_high[:, m, :], h1_sb[:, m, :], ACT.Copy).then_inc(h1_highs_formed, 1)

            def take2(q):
                act.wait_ge(h1_used, M1 * (q + 1))
                if q >= 2:
                    act.wait_ge(y_summed, q - 1)
                for m in range(M2):
                    nc.scalar.activation(h2_sb[:, q % 2, m, :], head_banks[M1 + m], ACT.Relu,
                                         bias=bt2_sb[:, m:m + 1]).then_inc(h2_ready, 1)

            act.wait_ge(splits_used, ALL.splits - 1)
            act.wait_ge(head_weights_in, 32)
            act.wait_ge(dense_in, 16)
            nc.scalar.activation(wt1_high, wt1_sb, ACT.Copy).then_inc(wt1_high_ready, 1)
            feat_highs(0)
            act.wait_ge(reduced1, i * HALVES + 2)
            evacuate1(i, L1_LAST)
            nc.scalar.activation(wt2_high, wt2_sb, ACT.Copy).then_inc(wt2_high_ready, 1)
            for q in range(QB):
                take1(q)
                if q + 1 < QB:
                    feat_highs(q + 1)
                take2(q)

        @block.vector
        def _(dve):
            def form(out, unit, left, right):
                def operand(tiles, indices):
                    if len(set(indices)) == 1:
                        one = tiles[:, indices[0], :].unsqueeze(1)
                        return one if len(indices) == 1 else one.broadcast_to([one.shape[0], 2, COLS])
                    return tiles[:, indices[0]:indices[1] + 1:indices[1] - indices[0], :]
                nc.vector.tensor_tensor(out[:, 0:len(unit), :], operand(left, [a for a, _ in unit]),
                                        operand(right, [b for _, b in unit]), ALU.mult).then_inc(units_formed, 1)

            def layer(steps, rows, left, right, done, turn, previous, arrived, between=()):
                recent = kinds(previous)
                plains = splits = formed = 0

                def slot_free():
                    last = recent[-NUNIT:]
                    if len(last) < NUNIT:
                        return
                    if last[0]:
                        dve.wait_ge(lows_formed, done.splits + (splits - sum(last[1:])))
                    else:
                        dve.wait_ge(plains_used, done.plains + (plains - (NUNIT - 1 - sum(last[1:]))))

                for step, (split_unit, plain_unit) in enumerate(steps):
                    if split_unit is not None:
                        arrived(split_unit)
                        slot_free()
                        whole = unit_ring[0:rows, (turn.units + formed) % NUNIT, 0:len(split_unit), :]
                        form(whole, split_unit, left, right)
                        formed += 1
                        splits += 1
                        recent.append(True)
                    arrived(plain_unit)
                    slot_free()
                    form(unit_ring[0:rows, (turn.units + formed) % NUNIT], plain_unit, left, right)
                    formed += 1
                    plains += 1
                    recent.append(False)
                    if split_unit is not None:
                        part = slice(0, len(split_unit))
                        slot = (turn.splits + splits - 1) % NSPLIT
                        dve.wait_ge(highs_formed, done.splits + splits)
                        nc.vector.tensor_tensor(low_ring[0:rows, slot, part, :], whole,
                                                high_ring[0:rows, slot, part, :].bitcast(F32),
                                                ALU.subtract).then_inc(lows_formed, 1)
                    if step >= REDUCE_AT and step - REDUCE_AT < len(between):
                        between[step - REDUCE_AT]()

            def layer0(i, turn, tile, h, previous=STEPS1):
                waited = set()

                def arrived(unit):
                    for j in sorted({j for pair in unit for j in pair} - waited):
                        dve.wait_ge(x_loaded[j], (tile * HALVES + h + 1) * 16)
                        waited.add(j)

                layer(STEPS0, P0, x_tiles, x_tiles, before(i, turn), turn, previous, arrived)

            def layer1(i, turn, h, between=(), previous=STEPS0):
                waited = set()

                def arrived(unit):
                    for k, j in unit:
                        if ("s", k) not in waited:
                            dve.wait_ge(s_loaded[h][k], (i + 1) * 16)
                        if ("t", j) not in waited:
                            dve.wait_ge(t_loaded[h][j], (i + 1) * 16)
                        waited.update((("s", k), ("t", j)))

                layer(STEPS1, P, s_tiles[:, h], t_tiles[:, h], before(i, turn), turn, previous,
                      arrived, between)

            def reduce_dims(rows, result, i, h, done):
                if h == 0:
                    dve.wait_ge(done, i * HALVES + 1)
                    rows, result = rows[:, 0:DH, :], rows[:, DH, :]
                else:
                    dve.wait_ge(done, i * HALVES + 2)
                nc.vector.tensor_reduce(result, rows.rearrange("p d b -> p b d"), AX_X, ALU.add).then_inc(done, 1)

            def reduce0(i, h):
                dve.wait_ge(l0_evacuated, i * HALVES + h + 1)
                reduce_dims(l0_out[H1:P], feat_b[H1:P, bass.ds(i * P, P)], i, h, reduced0)

            def reduce1(i, h):
                dve.wait_ge(l1_evacuated, i * HALVES + h + 2)
                reduce_dims(l1_out[:], feat_a[:, bass.ds(i * P, P)], i, h, reduced1)

            nc.vector.memset(feat_b[0:H1, :], 0.0).then_inc(feat_zeroed, 1)
            dve.wait_ge(consts_in, CONSTS_LANDED)
            nc.vector.tensor_tensor(w0_sb[:], w0_plain_in[:, 0], w0_plain_in[:, 1],
                                    ALU.add).then_inc(weights_summed, 1)
            nc.vector.tensor_tensor(w0_split_in[:, 0], w0_split_in[:, 0], w0_split_in[:, 1],
                                    ALU.add).then_inc(weights_summed, 1)
            dve.wait_ge(weights_high, 1)
            nc.vector.tensor_tensor(w1_low[:], w1_split_in, w1_high[:].bitcast(F32), ALU.subtract)\
                .then_inc(weights_split, 1)
            dve.wait_ge(weights_high, 2)
            nc.vector.tensor_tensor(w0_low[:], w0_split_in[:, 0], w0_high[:].bitcast(F32), ALU.subtract)\
                .then_inc(weights_split, 1)
            dve.wait_ge(weights_split, 2)
            dve.sem_inc(reduced1, 1)
            dve.sem_inc(reduced0, 1)
            layer0(0, PROLOGUE, 0, 0, previous=())
            layer0(0, L0_ODD, 0, 1, previous=STEPS0)
            reduce0(0, 0)
            layer1(0, L1_EVEN, 0, (lambda: reduce0(0, 1),))
            layer0(0, L0_EVEN, 1, 0)
            layer1(0, L1_ODD, 1, (lambda: reduce1(0, 0), lambda: reduce0(1, 0)))
            with dve.Fori(1, TILES - 1) as i:
                layer0(i, L0_ODD, i, 1)
                layer1(i, L1_EVEN, 0, (lambda: reduce1(i - 1, 1), lambda: reduce0(i, 1)))
                layer0(i, L0_EVEN, i + 1, 0)
                layer1(i, L1_ODD, 1, (lambda: reduce1(i, 0), lambda: reduce0(i + 1, 0)))
            i = TILES - 1
            layer0(i, L0_ODD, i, 1)
            layer1(i, L1_EVEN, 0, (lambda: reduce1(i - 1, 1), lambda: reduce0(i, 1)))
            layer1(i, L1_LAST, 1, (lambda: reduce1(i, 0),), previous=STEPS1)

            def feat_lows(q):
                for kt, feat in enumerate((feat_a, feat_b)):
                    dve.wait_ge(feat_highs_formed, 2 * q + kt + 1)
                    nc.vector.tensor_tensor(feat_low[:, kt, :], feat[:, q * BANK:(q + 1) * BANK],
                                            feat_high[:, kt, :].bitcast(F32),
                                            ALU.subtract).then_inc(feat_lows_formed, 1)

            def h1_lows(q):
                for m in range(M1):
                    dve.wait_ge(h1_highs_formed, M1 * q + m + 1)
                    nc.vector.tensor_tensor(h1_low[:, m, :], h1_sb[:, m, :], h1_high[:, m, :].bitcast(F32),
                                            ALU.subtract).then_inc(h1_lows_formed, 1)

            def take_y(q):
                dve.wait_ge(y_summed, q + 1)
                nc.vector.tensor_copy(y_sb[:, q * BANK:(q + 1) * BANK],
                                      head_banks[M1 + M2][0:1, :]).then_inc(y_ready, 1)

            dve.wait_ge(wt1_high_ready, 1)
            nc.vector.tensor_tensor(wt1_low, wt1_sb, wt1_high.bitcast(F32), ALU.subtract).then_inc(wt1_split, 1)
            feat_lows(0)
            reduce1(i, 1)
            dve.wait_ge(wt2_high_ready, 1)
            nc.vector.tensor_tensor(wt2_low, wt2_sb, wt2_high.bitcast(F32), ALU.subtract).then_inc(wt2_split, 1)
            for q in range(QB):
                h1_lows(q)
                if q + 1 < QB:
                    feat_lows(q + 1)
                if q > 0:
                    take_y(q - 1)
            take_y(QB - 1)


def shifts(j, r):
    base, step = SHIFT_BASE_STEP[j]
    return [(r + base + step * g) % F for g in range(GROUPS)]


def layer0_rows():
    pairs = PLAIN0 + SPLIT0
    forward = np.full((P0, len(pairs)), -1)
    backward = np.full((P0, len(pairs)), -1)
    seen = set()
    for n, (a, b) in enumerate(pairs):
        for r in range(F):
            for g, (h, m) in enumerate(zip(shifts(a, r), shifts(b, r))):
                if (min(h, m), max(h, m)) in seen:
                    continue
                seen.add((min(h, m), max(h, m)))
                forward[r * GROUPS + g, n] = h * F + m
                if h != m:
                    backward[r * GROUPS + g, n] = m * F + h
    assert len(seen) == F * (F + 1) // 2
    return forward, backward


def layer1_rows():
    pairs = PLAIN1 + SPLIT1
    place = np.full((P, len(pairs)), -1)
    for p in range(P):
        u, v = divmod(p, VX)
        for n, (k, j) in enumerate(pairs):
            if RX * v + k < F:
                place[p, n] = (RY * u + j) * F + RX * v + k
    return place


def rows_or_zero(w, place):
    laid = np.zeros(place.shape + (w.shape[0],), w.dtype)
    laid[place >= 0] = w.T[place[place >= 0]]
    return laid


def kernel(**inputs):
    import concourse.bacc as bacc
    from concourse.bass_utils import run_bass_kernel_spmd

    a = {name: np.asarray(x) for name, x in inputs.items()}
    forward, backward = layer0_rows()
    w0 = np.stack([rows_or_zero(a["L0_rec_W0"], place) for place in (forward, backward)], axis=1)
    w1 = rows_or_zero(a["L0_rec_W1"], layer1_rows())
    w_top1 = np.zeros((P, 2, HID1), a["W_top1"].dtype)
    w_top1[:, 0] = a["W_top1"][H1:H1 + OUT]
    w_top1[0:D, 1] = a["W_top1"][H1 + OUT:]
    w_top1[H1:, 1] = a["W_top1"][0:H1]
    arrays = {
        "dense_t": a["dense_ctx"].T,
        "ids": a["ids"].reshape(TILES, P, F),
        "w0_plain": w0[:, :, :len(PLAIN0)],
        "w0_split": w0[:, :, len(PLAIN0):],
        "b0": a["L0_rec_b0"].reshape(P, 1),
        "w1_plain": w1[:, :len(PLAIN1)],
        "w1_split": w1[:, len(PLAIN1):],
        "b1": a["L0_rec_b1"].reshape(P, 1),
        "wt1": w_top1,
        "bt1": a["b_top1"].reshape(M1, P).T,
        "wt2": a["W_top2"].reshape(M1, P, HID2).transpose(1, 0, 2),
        "bt2": a["b_top2"].reshape(M2, P).T,
        "wt3": a["W_top3"].reshape(M2, P).T,
        "ident": np.eye(P, dtype=np.float32),
    }
    arrays |= {f"tbl_{f}": a[f"tbl_{f}"] for f in range(F)}
    arrays = {f"in_{name}": np.ascontiguousarray(x) for name, x in arrays.items()}
    nc = bacc.Bacc("TRN2", target_bir_lowering=False, num_devices=1)
    aps = {name: nc.dram_tensor(name, x.shape, mybir.dt.from_np(x.dtype), kind="ExternalInput").ap()
           for name, x in arrays.items()}
    out = nc.dram_tensor("out_y", (B, 1), F32, kind="ExternalOutput").ap()
    names = ("dense_t", "ids", "w0_plain", "w0_split", "b0", "w1_plain", "w1_split", "b1",
             "wt1", "bt1", "wt2", "bt2", "wt3", "ident")
    interaction_kernel(nc, tables=[aps[f"in_tbl_{f}"] for f in range(F)], out=out,
                       **{name: aps[f"in_{name}"] for name in names})
    result = run_bass_kernel_spmd(nc, [arrays], core_ids=[0])
    return result.results[0]["out_y"]
```
